# Optimizing a Trainium2 kernel written in Bass

```python
import numpy as np
import jax
import jax.numpy as jnp

def _softmax(x, axis=-1):
    return jax.nn.softmax(x, axis=axis)

def _gelu(x):
    return jax.nn.gelu(x, approximate=True)

def _silu(x):
    return jax.nn.silu(x)

def _sigmoid(x):
    return jax.nn.sigmoid(x)

def _layernorm(x, axis=-1, eps=1e-05):
    m = jnp.mean(x, axis=axis, keepdims=True)
    v = jnp.var(x, axis=axis, keepdims=True)
    return (x - m) / jnp.sqrt(v + eps)

def _scatter_add(tgt, idx, src, axis=0):
    return tgt.at[idx].add(src)

def _segment_sum(src, seg, n):
    return jax.ops.segment_sum(src, seg, n)
kernel_name = 'mk_adj_ffn_d1_adj_r2_a705f4'

def setup_inputs(seed: int=0):
    np.random.seed(seed)
    _w = jnp.asarray

    def _rec_inputs():
        import jax
        import jax.numpy as jnp
        _gk = jax.random.key(seed)
        x = -0.0002928 + 1 * jax.random.normal(jax.random.fold_in(_gk, 1), (8, 1024, 128), jnp.float32)
        _a = jax.random.bernoulli(jax.random.fold_in(_gk, 2), 0.0078125, (8, 1024, 1024))
        adj = _a.astype(jnp.int32)
        return (x, adj)
    x, adj = _rec_inputs()

    def _L0_gnn_setup():
        import jax, jax.numpy as jnp
        import numpy as np
        OUT = 128
        NUM_LAYERS = 3

        def _gru_cell(inp, h, w_ih, w_hh, b_ih, b_hh):
            gi = inp @ w_ih.T + b_ih
            gh = h @ w_hh.T + b_hh
            i_r, i_z, i_n = jnp.split(gi, 3, axis=-1)
            h_r, h_z, h_n = jnp.split(gh, 3, axis=-1)
            r = jax.nn.sigmoid(i_r + h_r)
            z = jax.nn.sigmoid(i_z + h_z)
            n = jnp.tanh(i_n + r * h_n)
            return (1.0 - z) * n + z * h
        key = jax.random.key(seed)
        ks = jax.random.split(key, 8)
        B, N, D = (32, 256, 128)
        x = jax.random.normal(ks[0], (B, N, D), dtype=jnp.float32)
        adj = jax.random.randint(ks[1], (B, N, N), 0, 2, dtype=jnp.int32)
        s = 1.0 / np.sqrt(OUT)
        weight = jax.random.uniform(ks[2], (NUM_LAYERS, OUT, OUT), jnp.float32, -s, s)
        w_ih = jax.random.uniform(ks[3], (3 * OUT, OUT), jnp.float32, -s, s)
        w_hh = jax.random.uniform(ks[4], (3 * OUT, OUT), jnp.float32, -s, s)
        b_ih = jax.random.uniform(ks[5], (3 * OUT,), jnp.float32, -s, s)
        b_hh = jax.random.uniform(ks[6], (3 * OUT,), jnp.float32, -s, s)
        return {'x': x, 'adj': adj, 'weight': weight, 'w_ih': w_ih, 'w_hh': w_hh, 'b_ih': b_ih, 'b_hh': b_hh}
    _L0_gnn_all = _L0_gnn_setup()
    _L0_gnn_in = {k: v for k, v in _L0_gnn_all.items() if k in ('weight', 'w_ih', 'w_hh', 'b_ih', 'b_hh')}
    del _L0_gnn_all

    def _L0_ffn_setup():
        import jax, jax.numpy as jnp
        import numpy as np
        B, S, D, E, H, K = (4, 2048, 128, 8, 256, 2)
        key = jax.random.key(seed)
        ks = jax.random.split(key, 6)
        x = jax.random.normal(ks[0], (B, S, D), jnp.float32)
        Wg = jax.random.normal(ks[1], (D, E), jnp.float32) * 0.02
        bg = jnp.zeros((E,), jnp.float32)
        W1 = jax.random.normal(ks[2], (E, D, H), jnp.float32) * 0.02
        b1 = jnp.zeros((E, H), jnp.float32)
        W2 = jax.random.normal(ks[3], (E, H, D), jnp.float32) * 0.02
        b2 = jnp.zeros((E, D), jnp.float32)
        return {'x': x, 'Wg': Wg, 'bg': bg, 'W1': W1, 'b1': b1, 'W2': W2, 'b2': b2}
    _L0_ffn_all = _L0_ffn_setup()
    _L0_ffn_in = {k: v for k, v in _L0_ffn_all.items() if k in ('Wg', 'bg', 'W1', 'b1', 'W2', 'b2')}
    del _L0_ffn_all
    return {'x': x, 'adj': adj, 'L0_gnn_weight': _L0_gnn_in['weight'], 'L0_gnn_w_ih': _L0_gnn_in['w_ih'], 'L0_gnn_w_hh': _L0_gnn_in['w_hh'], 'L0_gnn_b_ih': _L0_gnn_in['b_ih'], 'L0_gnn_b_hh': _L0_gnn_in['b_hh'], 'L0_ffn_Wg': _L0_ffn_in['Wg'], 'L0_ffn_bg': _L0_ffn_in['bg'], 'L0_ffn_W1': _L0_ffn_in['W1'], 'L0_ffn_b1': _L0_ffn_in['b1'], 'L0_ffn_W2': _L0_ffn_in['W2'], 'L0_ffn_b2': _L0_ffn_in['b2']}

def reference(x, adj, L0_gnn_weight, L0_gnn_w_ih, L0_gnn_w_hh, L0_gnn_b_ih, L0_gnn_b_hh, L0_ffn_Wg, L0_ffn_bg, L0_ffn_W1, L0_ffn_b1, L0_ffn_W2, L0_ffn_b2):
    import jax
    import jax.numpy as jnp

    def _L0_gnn_ref(x, adj, weight, w_ih, w_hh, b_ih, b_hh):
        import jax, jax.numpy as jnp
        import numpy as np
        OUT = 128
        NUM_LAYERS = 3

        def _gru_cell(inp, h, w_ih, w_hh, b_ih, b_hh):
            gi = inp @ w_ih.T + b_ih
            gh = h @ w_hh.T + b_hh
            i_r, i_z, i_n = jnp.split(gi, 3, axis=-1)
            h_r, h_z, h_n = jnp.split(gh, 3, axis=-1)
            r = jax.nn.sigmoid(i_r + h_r)
            z = jax.nn.sigmoid(i_z + h_z)
            n = jnp.tanh(i_n + r * h_n)
            return (1.0 - z) * n + z * h
        A = (adj != 0).astype(x.dtype)
        h = x
        L = weight.shape[0]
        for i in range(L):
            m = jnp.einsum('bnd,de->bne', h, weight[i])
            aggr = jnp.einsum('bst,bsd->btd', A, m)
            h = _gru_cell(aggr, h, w_ih, w_hh, b_ih, b_hh)
        return h

    def _L0_ffn_ref(x, Wg, bg, W1, b1, W2, b2):
        import jax, jax.numpy as jnp
        import numpy as np
        B, S, D, E, H, K = (4, 2048, 128, 8, 256, 2)
        Bv, Sv, Dv = x.shape
        gate_scores = x @ Wg + bg
        _, idx = jax.lax.top_k(gate_scores, K)
        mask = jax.nn.one_hot(idx, E, dtype=x.dtype).sum(axis=-2)
        xf = x.reshape(-1, Dv)
        mf = mask.reshape(-1, E)
        h = jax.nn.gelu(jnp.einsum('td,edh->teh', xf, W1) + b1[None], approximate=False)
        y = jnp.einsum('teh,ehd->ted', h, W2) + b2[None]
        out = jnp.einsum('ted,te->td', y, mf)
        return out.reshape(Bv, Sv, Dv)
    x = x + _L0_gnn_ref(_layernorm(x, axis=-1), adj, L0_gnn_weight, L0_gnn_w_ih, L0_gnn_w_hh, L0_gnn_b_ih, L0_gnn_b_hh)
    x = x + _L0_ffn_ref(_layernorm(x, axis=-1), L0_ffn_Wg, L0_ffn_bg, L0_ffn_W1, L0_ffn_b1, L0_ffn_W2, L0_ffn_b2)
    return x

_drawn_inputs = setup_inputs


def setup_inputs(seed=0):
    import zlib

    import numpy as np

    out = dict(_drawn_inputs(seed))
    spreads = {'L0_ffn_bg': (0.0, 0.1), 'L0_ffn_b1': (0.0, 0.398), 'L0_ffn_b2': (0.0, 0.1)}
    factors = {}
    for name, (base, spread) in spreads.items():
        noise = np.random.default_rng([zlib.crc32(name.encode()), seed]).standard_normal(out[name].shape)
        drawn = base * np.exp(spread * noise) if base else spread * noise
        out[name] = jnp.asarray(drawn.astype(out[name].dtype))
    for name, factor in factors.items():
        out[name] = (out[name] * factor).astype(out[name].dtype)
    return out
```

```python
import concourse.bass as bass
from concourse import mybir
from contextlib import ExitStack

F32 = mybir.dt.float32
R32 = mybir.dt.float32r
I32 = mybir.dt.int32
ALU = mybir.AluOpType
ACT = mybir.ActivationFunctionType

P = 128
B = 8
N = 1024
T = N // P
LAYERS = 3
CH = 512
CT = CH // P
EPS = 1e-5
STG = 4


def f32(ap):
    return ap.bitcast(F32)


def need(eng, sem, value):
    if isinstance(value, int) and value <= 0:
        return
    eng.wait_ge(sem, value)


E = 8
HC = 2
J = E * HC
FAR = -1.0e30


def gnn_ffn(nc, x, adj, weight, w_ih, w_hh, b_ih, b_hh, Wg, bg, W1, b1, W2, b2, out):
    with ExitStack() as whole:
        def sb(name, shape, dt=F32):
            return whole.enter_context(nc.sbuf_tensor(name, shape, dt))

        def sem(name):
            return whole.enter_context(nc.semaphore(name))

        bank = [whole.enter_context(nc.psum_tensor(f"bank{i}", [P, CH], F32)) for i in range(8)]
        x2 = sb("x2", [P, B * T, P])
        ident = sb("ident", [P, P])
        mhalf = sb("mhalf", [P, T])
        bcol = sb("bcol", [P, 22])
        w1_raw = sb("w1_raw", [P, E, HC * P])
        w_raw_in = sem("w_raw_in")
        id_made = sem("id_made")
        graphs(nc, x, adj, weight, w_ih, w_hh, b_ih, b_hh, b1, W1, W2, bank, x2, ident, mhalf, bcol,
               w1_raw, w_raw_in, id_made, sem)
        experts(nc, Wg, bg, W2, b2, out, bank, x2, ident, mhalf, bcol, w1_raw, w_raw_in, sem)


def graphs(nc, x, adj, weight, w_ih, w_hh, b_ih, b_hh, b1, W1, W2, bank, x2, ident, mhalf, bcol,
           w1_raw, w_raw_in, id_made, sem):
    with ExitStack() as ctx:
        def sb(name, shape, dt=F32):
            return ctx.enter_context(nc.sbuf_tensor(name, shape, dt))

        AG = bank[0:2]
        R, Z, HN, IN = bank[2:6]
        TR = bank[6:8]
        stage = sb("stage", [P, STG, N], I32)
        A = [sb(f"A{i}", [P, T, N], R32) for i in range(2)]
        hT = [sb(f"hT{i}", [P, 2, CH]) for i in range(2)]
        hT_hi = [sb(f"hT_hi{i}", [P, 2, CH], R32) for i in range(2)]
        hT_lo = [sb(f"hT_lo{i}", [P, 2, CH], R32) for i in range(2)]
        hN_hi = [sb(f"hN_hi{i}", [P, T, P], R32) for i in range(2)]
        hN_lo = [sb(f"hN_lo{i}", [P, T, P], R32) for i in range(2)]
        ag_hi = [sb(f"ag_hi{i}", [P, CH], R32) for i in range(2)]
        ag_lo = [sb(f"ag_lo{i}", [P, CH], R32) for i in range(2)]
        rt = [sb(f"rt{i}", [P, CH]) for i in range(2)]
        zt = [sb(f"zt{i}", [P, CH]) for i in range(2)]
        zh = [sb(f"zh{i}", [P, CH]) for i in range(2)]
        xin = [sb(f"xin{i}", [P, T, P]) for i in range(2)]
        xn = sb("xn", [P, T, P])
        stats = sb("stats", [P, T, 6])
        mv = sb("mv", [P, T, 2])
        veps = sb("veps", [P, T])
        rstd = sb("rstd", [P, T])
        wi_hi = sb("wi_hi", [P, LAYERS, 3, P], R32)
        wi_lo = sb("wi_lo", [P, LAYERS, 3, P], R32)
        wh_hi = sb("wh_hi", [P, 3, P], R32)
        wh_lo = sb("wh_lo", [P, 3, P], R32)
        brz = sb("brz", [P, 2])
        w_raw = rt[0][:, 0:384].rearrange("p (i e) -> p i e", i=3)
        wih_raw = rt[1][:, 0:384].rearrange("p (i e) -> p i e", i=3)
        whh_raw = zt[0][:, 0:384].rearrange("p (i e) -> p i e", i=3)
        wT = zt[1][:, 0:384].rearrange("p (i e) -> p i e", i=3)
        wihT = zh[0][:, 0:384]
        brow = zh[1][0:22, 0:P]

        dve_passed = sem("dve_passed")
        w_loaded = sem("w_loaded")
        w_turned = sem("w_turned")
        w_taken = sem("w_taken")
        w_fused = sem("w_fused")
        w_split = sem("w_split")
        stage_in = [sem(f"stage_in{i}") for i in range(STG)]
        a_made = sem("a_made")
        x_in = [sem(f"x_in{i}") for i in range(2)]
        ln_stats = sem("ln_stats")
        ln_mv = sem("ln_mv")
        ln_veps = sem("ln_veps")
        ln_rstd = sem("ln_rstd")
        ln_xn = sem("ln_xn")
        prep_hi = sem("prep_hi")
        prep_lo = sem("prep_lo")
        prep_t = sem("prep_t")
        tr_full = sem("tr_full")
        tr_free = sem("tr_free")
        tok_hi = sem("tok_hi")
        ag_full = sem("ag_full")
        ag_his = sem("ag_his")
        ag_los = sem("ag_los")
        r_full = sem("r_full")
        z_full = sem("z_full")
        hn_full = sem("hn_full")
        in_full = sem("in_full")
        r_done = sem("r_done")
        z_done = sem("z_done")
        t_done = sem("t_done")
        t2_done = sem("t2_done")
        n_done = sem("n_done")
        v_done = sem("v_done")
        zh_done = sem("zh_done")
        h_done = sem("h_done")
        hhi_done = sem("hhi_done")
        hlo_done = sem("hlo_done")

        def chunk_no(it, half, l, c):
            return 12 * it + 6 * half + 2 * l + c

        def tr_no(it, half, k):
            return 16 * it + 8 * half + k

        def loop(eng, pair):
            pair(0)
            with eng.Fori(1, B // 2 - 1) as it:
                pair(it)
            pair(B // 2 - 1)

        def is_last(it, half):
            return half == 1 and isinstance(it, int) and it == B // 2 - 1

        def is_first(it, half):
            return half == 0 and isinstance(it, int) and it == 0

        def hidden(l, what, half=None):
            return what[0] if l == 0 else what[1]

        block = ctx.enter_context(nc.Block())

        @block.sync
        def _(sp):
            xv = x.rearrange("b (t p) d -> b p t d", p=P)
            av = adj.rearrange("b (t p) n -> b t p n", p=P)

            def rows(b, t, n):
                need(sp, a_made, n - STG + 1)
                sp.dma_start(stage[:, t % STG, :], av[b, t, :, :] if isinstance(b, int)
                             else av[bass.ds(b, 1), t, :, :].rearrange("o p n -> (o p) n")).then_inc(stage_in[t % STG], 16)

            for t in range(T):
                rows(0, t, t)

            def pair(it):
                for half in range(2):
                    if is_last(it, half):
                        continue
                    nxt = 2 * it + half + 1
                    if not is_first(it, half):
                        sp.wait_ge(tr_free, 8 * (nxt - 1) + 2)
                    sp.dma_start(xin[(half + 1) % 2][:, :, :], xv[nxt, :, :, :] if isinstance(nxt, int)
                                 else xv[bass.ds(nxt, 1), :, :, :].rearrange("o p t d -> (o p) t d")).then_inc(x_in[(half + 1) % 2], 16)
                    for t in range(T):
                        rows(nxt, t, 8 * nxt + t)

            loop(sp, pair)
            sp.dma_start(w1_raw[:, :, :], W1.rearrange("e d h -> d e h")).then_inc(w_raw_in, 16)

        @block.gpsimd
        def _(pool):
            nc.gpsimd.memset(mhalf[:, :], -0.5).then_inc(id_made, 1)
            nc.gpsimd.memset(ident[:, :], 0.0).then_inc(id_made, 1)
            pool.wait_ge(id_made, 2)
            nc.gpsimd.affine_select(out=ident[:, :], in_=ident[:, :], compare_op=ALU.not_equal, fill=1.0,
                                    base=0, pattern=[[-1, P]], channel_multiplier=1).then_inc(id_made, 1)

            def input_scale(nb):
                pool.wait_ge(ln_veps, nb + 1)
                nc.gpsimd.tensor_tensor(rstd[:, :], veps[:, :], mhalf[:, :], ALU.pow).then_inc(ln_rstd, 1)

            def input_lo(nb):
                pool.wait_ge(prep_hi, nb + 1)
                need(pool, ag_full, 6 * (nb - 1) + 2)
                nc.gpsimd.tensor_tensor(hN_lo[0][:, :, :], xn[:, :, :], f32(hN_hi[0][:, :, :]),
                                        ALU.subtract).then_inc(prep_lo, 1)

            input_scale(0)
            input_lo(0)
            def keep(it, half, l, c):
                n = chunk_no(it, half, l, c)
                pool.wait_ge(z_done, n + 1)
                if l == 0:
                    pool.wait_ge(prep_t, 4 * (2 * it + half) + 4)
                else:
                    pool.wait_ge(h_done, n - 1)
                need(pool, h_done, n - 1)
                nc.gpsimd.tensor_tensor(zh[c][:, :], zt[c][:, :], hidden(l, hT)[:, c, :],
                                        ALU.mult).then_inc(zh_done, 1)

            def pair(it):
                for half in range(2):
                    more = not is_last(it, half)
                    nb = 2 * it + half + 1
                    for l in range(LAYERS):
                        for c in range(2):
                            keep(it, half, l, c)
                            if more and l == 0 and c == 0:
                                input_scale(nb)
                        if l == 1 and more:
                            input_lo(nb)

            loop(pool, pair)

        @block.scalar
        def _(act):
            act.dma_start(xin[0][:, :, :], x.rearrange("b (t p) d -> b p t d", p=P)[0, :, :, :]).then_inc(x_in[0], 16)
            act.dma_start(w_raw, weight.rearrange("i d e -> d i e")).then_inc(w_loaded, 16)
            act.dma_start(wih_raw, w_ih.rearrange("(i j) e -> j i e", j=P)).then_inc(w_loaded, 16)
            act.dma_start(whh_raw, w_hh.rearrange("(i j) e -> j i e", j=P)).then_inc(w_loaded, 16)
            act.dma_start(brow[0:3, :], b_ih.rearrange("(i j) -> i j", j=P)).then_inc(w_loaded, 16)
            act.dma_start(brow[3:6, :], b_hh.rearrange("(i j) -> i j", j=P)).then_inc(w_loaded, 16)
            act.dma_start(brow[6:22, :], b1.rearrange("e (c j) -> (e c) j", j=P)).then_inc(w_loaded, 16)

            def input_hi(nb):
                act.wait_ge(ln_xn, nb + 1)
                need(act, ag_full, 6 * (nb - 1) + 2)
                nc.scalar.activation(hN_hi[0][:, :, :], xn[:, :, :], ACT.Copy).then_inc(prep_hi, 1)

            def input_turned(nb, c, tr, k):
                act.wait_ge(tr_full, tr + 1)
                need(act, zh_done, 6 * (nb - 1) + c + 1)
                need(act, hn_full, 6 * (nb - 1) + c + 1)
                nc.scalar.activation(hT[0][:, c, :], TR[k % 2][:, :], ACT.Copy).then_inc(prep_t, 1)
                nc.scalar.activation(hT_hi[0][:, c, :], TR[k % 2][:, :], ACT.Copy).then_inc(prep_t, 1)

            input_hi(0)
            for c in range(2):
                input_turned(0, c, c, c)

            def node_major_hi(it, half, l, c):
                n = chunk_no(it, half, l, c)
                k = {0: 2, 1: 4}[l] + c
                act.wait_ge(tr_full, tr_no(it, half, k) + 1)
                if c == 0:
                    act.wait_ge(ag_full, n + 2)
                nc.scalar.activation(hN_hi[1][:, CT * c:CT * c + CT, :], TR[k % 2][:, :].rearrange("p (t d) -> p t d", t=CT),
                                     ACT.Copy).then_inc(tok_hi, 1)

            def pair(it):
                for half in range(2):
                    for l in range(LAYERS):
                        for c in range(2):
                            n = chunk_no(it, half, l, c)
                            act.wait_ge(ag_full, n + 1)
                            need(act, in_full, n - 1)
                            nc.scalar.activation(ag_hi[c][:, :], AG[c][:, :], ACT.Copy).then_inc(ag_his, 1)
                        if l == 2 and not is_last(it, half):
                            nb = 2 * it + half + 1
                            for c in range(2):
                                input_turned(nb, c, tr_no(it, half, 6 + c), 6 + c)
                        for c in range(2):
                            n = chunk_no(it, half, l, c)
                            act.wait_ge(r_full, n + 1)
                            need(act, h_done, n - 1)
                            if is_first(it, half) and l == 0:
                                act.wait_ge(w_split, 4)
                            nc.scalar.activation(rt[c][:, :], R[:, :], ACT.Sigmoid, bias=brz[:, 0:1]).then_inc(r_done, 1)
                            act.wait_ge(z_full, n + 1)
                            nc.scalar.activation(zt[c][:, :], Z[:, :], ACT.Sigmoid, bias=brz[:, 1:2]).then_inc(z_done, 1)
                            if c == 1 and l < 2:
                                node_major_hi(it, half, l, 0)
                            act.wait_ge(t2_done, n + 1)
                            nc.scalar.activation(rt[c][:, :], rt[c][:, :], ACT.Tanh, bias=bcol[:, 2:3]).then_inc(n_done, 1)
                        if l < 2:
                            node_major_hi(it, half, l, 1)
                        if l == 1 and not is_last(it, half):
                            input_hi(2 * it + half + 1)

            loop(act, pair)

        @block.vector
        def _(dve):
            def input_norm(half, nb):
                dve.wait_ge(x_in[half], 16 * (nb // 2 + 1) if isinstance(nb, int) else 8 * (nb - half) + 16)
                for t in range(T):
                    ins = nc.vector.bn_stats(stats[:, t, :], xin[half][:, t, :])
                ins.then_inc(ln_stats, 1)
                dve.wait_ge(ln_stats, nb + 1)
                dve.sem_inc(dve_passed, 1)
                for t in range(T):
                    ins = nc.vector.bn_aggr(mv[:, t, :], stats[:, t, :])
                ins.then_inc(ln_mv, 1)
                dve.wait_ge(ln_mv, nb + 1)
                nc.vector.tensor_scalar(veps[:, :], mv[:, :, 1], EPS, None, ALU.add).then_inc(ln_veps, 1)

            def input_apply(half, nb):
                dve.wait_ge(ln_rstd, nb + 1)
                need(dve, prep_lo, nb)
                need(dve, prep_t, 4 * nb)
                for t in range(T):
                    ins = nc.vector.tensor_scalar(xn[:, t, :], xin[half][:, t, :], mv[:, t, 0:1], rstd[:, t:t + 1],
                                                  ALU.subtract, ALU.mult)
                ins.then_inc(ln_xn, 1)

            def convert(half, t, nb):
                dve.wait_ge(stage_in[t % STG], 16 * (2 * nb + t // STG + 1))
                if t == 0:
                    need(dve, ag_full, 6 * (nb - 1))
                nc.vector.tensor_scalar(A[half][:, t, :], stage[:, t % STG, :], 0, None,
                                        ALU.not_equal).then_inc(a_made, 1)

            def input_turned_lo(nb, c, k):
                dve.wait_ge(prep_t, 4 * nb + 2 * c + 2)
                need(dve, hn_full, 6 * (nb - 1) + c + 1)
                nc.vector.tensor_tensor(hT_lo[0][:, c, :], TR[k % 2][:, :], f32(hT_hi[0][:, c, :]),
                                        ALU.subtract).then_inc(tr_free, 1)

            input_norm(0, 0)
            dve.wait_ge(w_turned, 4)
            nc.vector.tensor_copy(wT, AG[0][:, 0:384].rearrange("p (i e) -> p i e", i=3)).then_inc(w_taken, 1)
            nc.vector.tensor_copy(wihT, AG[1][:, 0:384]).then_inc(w_taken, 1)
            nc.vector.tensor_copy(bcol[:, :], Z[:, 0:22]).then_inc(w_taken, 1)
            nc.vector.tensor_copy(wh_hi[:, :, :], R[:, 0:384].rearrange("p (i e) -> p i e", i=3)).then_inc(w_taken, 1)
            dve.wait_ge(w_taken, 4)
            nc.vector.tensor_tensor(brz[:, :], bcol[:, 0:2], bcol[:, 3:5], ALU.add).then_inc(w_split, 1)
            nc.vector.tensor_tensor(wh_lo[:, :, :], R[:, 0:384].rearrange("p (i e) -> p i e", i=3),
                                    f32(wh_hi[:, :, :]), ALU.subtract).then_inc(w_split, 1)
            fused = [HN, IN, AG[0]]
            input_apply(0, 0)
            dve.wait_ge(w_fused, 1)
            for l in range(LAYERS):
                src = fused[l][:, 0:384].rearrange("p (i e) -> p i e", i=3)
                ins = nc.vector.tensor_copy(wi_hi[:, l, :, :], src)
            ins.then_inc(w_split, 1)
            dve.wait_ge(w_split, 3)
            for l in range(LAYERS):
                src = fused[l][:, 0:384].rearrange("p (i e) -> p i e", i=3)
                ins = nc.vector.tensor_tensor(wi_lo[:, l, :, :], src, f32(wi_hi[:, l, :, :]), ALU.subtract)
            ins.then_inc(w_split, 1)
            for c in range(2):
                input_turned_lo(0, c, c)
            for t in range(T):
                convert(0, t, 0)

            def node_major_lo(it, half, l, c):
                n = chunk_no(it, half, l, c)
                k = {0: 2, 1: 4}[l] + c
                dve.wait_ge(tok_hi, 8 * it + 4 * half + 2 * l + c + 1)
                nc.vector.tensor_tensor(hN_lo[1][:, CT * c:CT * c + CT, :], TR[k % 2][:, :].rearrange("p (t d) -> p t d", t=CT),
                                        f32(hN_hi[1][:, CT * c:CT * c + CT, :]), ALU.subtract).then_inc(tr_free, 1)

            def residual(it, half, c, k, tr):
                dve.wait_ge(tr_full, tr + 1)
                at = 16 * it + 8 * half + CT * c
                dst = x2[:, at:at + CT, :] if isinstance(at, int) else x2[:, bass.ds(at, CT), :]
                nc.vector.tensor_tensor(dst, TR[k % 2][:, :].rearrange("p (t d) -> p t d", t=CT),
                                        xin[half][:, CT * c:CT * c + CT, :], ALU.add).then_inc(tr_free, 1)

            def pair(it):
                for half in range(2):
                    more = not is_last(it, half)
                    nb = 2 * it + half + 1
                    for l in range(LAYERS):
                        if l == 0 and not is_first(it, half):
                            pit, phalf = (it, 0) if half else (it - 1, 1)
                            for c in range(2):
                                residual(pit, phalf, c, c, tr_no(it, half, c))
                        for c in range(2):
                            n = chunk_no(it, half, l, c)
                            dve.wait_ge(ag_his, n + 1)
                            nc.vector.tensor_tensor(ag_lo[c][:, :], AG[c][:, :], f32(ag_hi[c][:, :]),
                                                    ALU.subtract).then_inc(ag_los, 1)
                        if more:
                            if l == 0:
                                input_norm((half + 1) % 2, nb)
                            if l == 2:
                                for c in range(2):
                                    input_turned_lo(nb, c, c)
                        for c in range(2):
                            n = chunk_no(it, half, l, c)
                            dve.wait_ge(r_done, n + 1)
                            dve.wait_ge(hn_full, n + 1)
                            nc.vector.scalar_tensor_tensor(out=rt[c][:, :], in0=HN[:, :], scalar=bcol[:, 5:6],
                                                           in1=rt[c][:, :], op0=ALU.add, op1=ALU.mult).then_inc(t_done, 1)
                            dve.wait_ge(t_done, n + 1)
                            dve.wait_ge(in_full, n + 1)
                            nc.vector.tensor_tensor(rt[c][:, :], IN[:, :], rt[c][:, :], ALU.add).then_inc(t2_done, 1)
                            if c == 1 and l < 2:
                                node_major_lo(it, half, l, 0)
                            if more:
                                for t in [[0], [1, 2], [3], [4, 5], [6], [7]][2 * l + c]:
                                    convert((half + 1) % 2, t, nb)
                            dve.wait_ge(n_done, n + 1)
                            dve.wait_ge(z_done, n + 1)
                            nc.vector.scalar_tensor_tensor(out=rt[c][:, :], in0=zt[c][:, :], scalar=1.0, in1=rt[c][:, :],
                                                           op0=ALU.subtract, op1=ALU.mult).then_inc(v_done, 1)
                            dve.wait_ge(v_done, n + 1)
                            dve.wait_ge(zh_done, n + 1)
                            nc.vector.tensor_tensor(hT[1][:, c, :], zh[c][:, :], rt[c][:, :],
                                                    ALU.subtract).then_inc(h_done, 1)
                            if l < 2:
                                dve.wait_ge(h_done, n + 1)
                                nc.vector.tensor_copy(hT_hi[1][:, c, :], hT[1][:, c, :]).then_inc(hhi_done, 1)
                                dve.wait_ge(hhi_done, 8 * it + 4 * half + 2 * l + c + 1)
                                nc.vector.tensor_tensor(hT_lo[1][:, c, :], hT[1][:, c, :], f32(hT_hi[1][:, c, :]),
                                                        ALU.subtract).then_inc(hlo_done, 1)
                        if l < 2:
                            node_major_lo(it, half, l, 1)
                        if l == 0 and more:
                            input_apply((half + 1) % 2, nb)

            loop(dve, pair)
            for c in range(2):
                residual(B // 2 - 1, 1, c, c, 8 * B - 2 + c)

        @block.tensor
        def _(pe):
            pe.wait_ge(id_made, 3)
            pe.wait_ge(w_loaded, 16 * 6)
            for dst, src in ((AG[0], w_raw), (AG[1], wih_raw), (R, whh_raw)):
                for i in range(3):
                    ins = nc.tensor.transpose(dst[:, P * i:P * i + P], src[:, i, :], ident[:, :])
                ins.then_inc(w_turned, 1)
            nc.tensor.transpose(Z[:, 0:22], brow, ident[0:22, 0:22]).then_inc(w_turned, 1)
            pe.wait_ge(w_taken, 2)
            for l, dst in enumerate((HN, IN, AG[0])):
                ins = nc.tensor.matmul(dst[:, 0:384], wT[:, l, :], wihT, start=True, stop=True)
            ins.then_inc(w_fused, 1)

            def input_turn(nb, c, tr, k):
                pe.wait_ge(ln_xn, nb + 1)
                need(pe, tr_free, tr - 1)
                for t in range(CT):
                    ins = nc.tensor.transpose(TR[k % 2][:, P * t:P * t + P], xn[:, CT * c + t, :], ident[:, :])
                ins.then_inc(tr_full, 1)

            def output_turn(n, c, tr, k):
                pe.wait_ge(h_done, n + 1)
                need(pe, tr_free, tr - 1)
                for t in range(CT):
                    ins = nc.tensor.transpose(TR[k % 2][:, P * t:P * t + P], hT[1][:, c, P * t:P * t + P], ident[:, :])
                ins.then_inc(tr_full, 1)

            def aggregate(it, half, l, c, part):
                n = chunk_no(it, half, l, 0)
                g = half
                for t in range(CT * part, CT * part + CT):
                    for h in (hidden(l, hN_hi), hidden(l, hN_lo)):
                        ins = nc.tensor.matmul(AG[c][:, :], h[:, t, :], A[g][:, t, CH * c:CH * c + CH],
                                               start=(t == 0 and h is hidden(l, hN_hi)),
                                               stop=(t == T - 1 and h is hidden(l, hN_lo)))
                if part == 1:
                    ins.then_inc(ag_full, 1)

            def products(dst, w_hi, w_lo, r_hi, r_lo, start, stop):
                for i, (w, r) in enumerate(((w_hi, r_hi), (w_hi, r_lo), (w_lo, r_hi))):
                    ins = nc.tensor.matmul(dst[:, :], w, r, start=(start and i == 0), stop=(stop and i == 2))
                return ins

            def from_h(it, half, l, c):
                n = chunk_no(it, half, l, c)
                b = 2 * it + half
                if l == 0:
                    pe.wait_ge(prep_t, 4 * b + 2 * c + 2)
                else:
                    pe.wait_ge(hlo_done, 8 * it + 4 * half + 2 * (l - 1) + c + 1)
                r_hi, r_lo = hidden(l, hT_hi)[:, c, :], hidden(l, hT_lo)[:, c, :]
                need(pe, r_done, n)
                products(R, wh_hi[:, 0, :], wh_lo[:, 0, :], r_hi, r_lo, True, False)
                need(pe, z_done, n)
                products(Z, wh_hi[:, 1, :], wh_lo[:, 1, :], r_hi, r_lo, True, False)
                need(pe, t_done, n)
                products(HN, wh_hi[:, 2, :], wh_lo[:, 2, :], r_hi, r_lo, True, True).then_inc(hn_full, 1)

            def from_ag(it, half, l, c):
                n = chunk_no(it, half, l, c)
                pe.wait_ge(ag_los, n + 1)
                r_hi, r_lo = ag_hi[c][:, :], ag_lo[c][:, :]
                products(R, wi_hi[:, l, 0, :], wi_lo[:, l, 0, :], r_hi, r_lo, False, True).then_inc(r_full, 1)
                products(Z, wi_hi[:, l, 1, :], wi_lo[:, l, 1, :], r_hi, r_lo, False, True).then_inc(z_full, 1)
                need(pe, t2_done, n)
                products(IN, wi_hi[:, l, 2, :], wi_lo[:, l, 2, :], r_hi, r_lo, True, True).then_inc(in_full, 1)

            for c in range(2):
                input_turn(0, c, c, c)
            pe.wait_ge(w_split, 4)

            def pair(it):
                for half in range(2):
                    b = 2 * it + half
                    for l in range(LAYERS):
                        n = chunk_no(it, half, l, 0)
                        if l > 0:
                            output_turn(n - 2, 0, tr_no(it, half, 2 if l == 1 else 4), 0)
                        if l == 0:
                            need(pe, tr_free, 8 * b if not is_first(it, half) else 2)
                        from_h(it, half, l, 0)
                        if l == 0:
                            pe.wait_ge(prep_lo, b + 1)
                            pe.wait_ge(a_made, 8 * b + CT)
                        else:
                            pe.wait_ge(tr_free, tr_no(it, half, 2 if l == 1 else 4) + 1)
                        for c in range(2):
                            need(pe, ag_los, n - 1 + c)
                            aggregate(it, half, l, c, 0)
                        if l > 0:
                            output_turn(n - 1, 1, tr_no(it, half, 3 if l == 1 else 5), 1)
                        elif not is_first(it, half):
                            for c in range(2):
                                output_turn(n - 2 + c, c, tr_no(it, half, c), c)
                        if l == 0:
                            pe.wait_ge(a_made, 8 * b + T)
                        else:
                            pe.wait_ge(tr_free, tr_no(it, half, 3 if l == 1 else 5) + 1)
                        aggregate(it, half, l, 0, 1)
                        aggregate(it, half, l, 1, 1)
                        if l == 2 and not is_last(it, half):
                            for c in range(2):
                                input_turn(b + 1, c, tr_no(it, half, 6 + c), c)
                        from_ag(it, half, l, 0)
                        from_h(it, half, l, 1)
                        from_ag(it, half, l, 1)

            loop(pe, pair)
            for c in range(2):
                output_turn(6 * B - 2 + c, c, 8 * B - 2 + c, c)


def experts(nc, Wg, bg, W2, b2, out, bank, x2, ident, mhalf, bcol, w1_raw, w_raw_in, sem):
    NQ = B * N // CH
    with ExitStack() as ctx:
        def sb(name, shape, dt=F32):
            return ctx.enter_context(nc.sbuf_tensor(name, shape, dt))

        U = bank[0:3]
        Y, XT, SC, NT, OT = bank[3:8]
        w2_raw = sb("w2_raw", [P, J, P])
        w1_hi = sb("w1_hi", [P, E, HC * P], R32)
        w1_lo = sb("w1_lo", [P, E, HC * P], R32)
        w2_hi = sb("w2_hi", [P, J, P], R32)
        w2_lo = sb("w2_lo", [P, J, P], R32)
        wg = sb("wg", [P, E])
        bg_row = sb("bg_row", [1, E])
        bgb = sb("bgb", [P, E])
        b2_raw = sb("b2_raw", [E, P])
        b2_hi = sb("b2_hi", [E, P], R32)
        b2_lo = sb("b2_lo", [E, P], R32)
        ones = sb("ones", [1, P])
        far_raw = sb("far_raw", [E, E, P])
        far = sb("far", [E, E, P], R32)
        before = sb("before", [P, E, E])
        stats = sb("f_stats", [P, CT, 6])
        mv = sb("f_mv", [P, CT, 2])
        veps = sb("f_veps", [P, CT])
        rstd = sb("f_rstd", [P, CT])
        xn = sb("f_xn", [P, CT, P])
        xT = sb("f_xT", [P, CH])
        xT_hi = [sb(f"xT_hi{i}", [P, CH], R32) for i in range(2)]
        xT_lo = [sb(f"xT_lo{i}", [P, CH], R32) for i in range(2)]
        sc = sb("sc", [P, CT, E])
        ge = sb("ge", [P, CT, E, E])
        gt = sb("gt", [P, CT, E, E])
        rank = sb("rank", [P, CT, E])
        unsel = sb("unsel", [P, CT, E])
        unselT = [sb(f"unselT{i}", [E, CH], R32) for i in range(2)]
        selT = [sb(f"selT{i}", [E, CH], R32) for i in range(2)]
        g = [sb(f"g{i}", [P, CH]) for i in range(4)]
        g_hi = [sb(f"g_hi{i}", [P, CH], R32) for i in range(4)]
        g_lo = [sb(f"g_lo{i}", [P, CH], R32) for i in range(4)]
        yT = sb("yT", [P, CH])
        yo = [sb(f"yo{i}", [P, CT, P]) for i in range(2)]

        small_in = sem("small_in")
        consts = sem("consts")
        bg_full = sem("bg_full")
        wsplit = sem("wsplit")
        s_stats = sem("s_stats")
        s_mv = sem("s_mv")
        s_veps = sem("s_veps")
        s_rstd = sem("s_rstd")
        s_xn = sem("s_xn")
        xt_full = sem("xt_full")
        xt_out = sem("xt_out")
        xt_lo = sem("xt_lo")
        sc_full = sem("sc_full")
        gate = sem("gate")
        nt_full = sem("nt_full")
        seled = sem("seled")
        u_full = sem("u_full")
        g_made = sem("g_made")
        g_his = sem("g_his")
        g_los = sem("g_los")
        down = sem("down")
        y_full = sem("y_full")
        y_out = sem("y_out")
        ot_full = sem("ot_full")
        yo_made = sem("yo_made")
        yo_stored = [sem(f"yo_stored{i}") for i in range(2)]
        held = sem("held")

        block = ctx.enter_context(nc.Block())
        outv = out.rearrange("b (q t p) d -> (b q) p t d", p=P, t=CT)

        def at(ap, q):
            return ap[CT * q:CT * q + CT] if isinstance(q, int) else ap

        def rows(q, t0, n):
            return x2[:, CT * q + t0:CT * q + t0 + n, :] if isinstance(q, int) else x2[:, bass.ds(CT * q + t0, n), :]

        def loop(eng, step):
            for k in range(2):
                step(k, k)
            with eng.Fori(1, NQ // 2 - 1) as i:
                for k in range(2):
                    step(2 * i + k, k)
            for k in range(2):
                step(NQ - 2 + k, k)

        def last(q):
            return isinstance(q, int) and q == NQ - 1

        @block.sync
        def _(sp):
            sp.dma_start(w2_raw[:, :, :], W2.rearrange("e (c h) d -> h (e c) d", h=P)).then_inc(w_raw_in, 16)
            sp.dma_start(wg[:, :], Wg).then_inc(small_in, 16)
            sp.dma_start(bg_row[:, :], bg.rearrange("(o e) -> o e", o=1)).then_inc(small_in, 16)
            sp.dma_start(b2_raw[:, :], b2).then_inc(small_in, 16)

            def step(q, k):
                sp.wait_ge(yo_made, q + 1)
                dst = outv[q, :, :, :] if isinstance(q, int) else outv[bass.ds(q, 1), :, :, :].rearrange("o p t d -> (o p) t d")
                sp.dma_start(dst, yo[k][:, :, :]).then_inc(yo_stored[k], 16)

            loop(sp, step)
            for k in range(2):
                sp.wait_ge(yo_stored[k], 16 * (NQ // 2))

        @block.gpsimd
        def _(pool):
            nc.gpsimd.memset(ones[:, :], 1.0).then_inc(consts, 1)
            nc.gpsimd.memset(far_raw[:, :, :], 0.0).then_inc(consts, 1)
            nc.gpsimd.memset(before[:, :, :], 1.0).then_inc(consts, 1)
            pool.wait_ge(consts, 3)
            nc.gpsimd.affine_select(out=far_raw[:, :, :], in_=far_raw[:, :, :], compare_op=ALU.not_equal, fill=FAR,
                                    base=0, pattern=[[-1, E], [0, P]], channel_multiplier=1).then_inc(consts, 1)
            nc.gpsimd.affine_select(out=before[:, :, :], in_=before[:, :, :], compare_op=ALU.is_gt, fill=0.0,
                                    base=0, pattern=[[1, E], [-1, E]], channel_multiplier=0).then_inc(consts, 1)

            def scale(q):
                pool.wait_ge(s_veps, q + 1)
                nc.gpsimd.tensor_tensor(rstd[:, :], veps[:, :], mhalf[:, 0:CT], ALU.pow).then_inc(s_rstd, 1)

            scale(0)

            def step(q, k):
                if not last(q):
                    scale(q + 1)

            loop(pool, step)

        @block.scalar
        def _(act):
            def x_out(q, k):
                act.wait_ge(xt_full, q + 1)
                need(act, sc_full, q)
                nc.scalar.activation(xT[:, :], XT[:, :], ACT.Copy).then_inc(xt_out, 1)
                need(act, u_full, J * (q - 1))
                nc.scalar.activation(xT_hi[k][:, :], XT[:, :], ACT.Copy).then_inc(xt_out, 1)

            def gelu(q, j):
                n = J * q + j
                act.wait_ge(u_full, n + 1)
                need(act, g_los, n - 3)
                nc.scalar.activation(g[j % 4][:, :], U[j % 2][:, :], ACT.Gelu, bias=bcol[:, 6 + j:7 + j]).then_inc(g_made, 1)

            def high(q, j):
                n = J * q + j
                act.wait_ge(g_made, n + 1)
                need(act, down, n - 3)
                nc.scalar.activation(g_hi[j % 4][:, :], g[j % 4][:, :], ACT.Copy).then_inc(g_his, 1)

            x_out(0, 0)

            def step(q, k):
                for j in range(J):
                    gelu(q, j)
                    if j > 0:
                        high(q, j - 1)
                    if j == 8 and not last(q):
                        x_out(q + 1, 1 - k)
                high(q, J - 1)
                act.wait_ge(y_full, q + 1)
                need(act, ot_full, q)
                nc.scalar.activation(yT[:, :], Y[:, :], ACT.Copy).then_inc(y_out, 1)

            loop(act, step)

        @block.vector
        def _(dve):
            def norm(q):
                for t in range(CT):
                    ins = nc.vector.bn_stats(stats[:, t, :], rows(q, t, 1).rearrange("p o d -> p (o d)"))
                ins.then_inc(s_stats, 1)
                dve.wait_ge(s_stats, q + 1)
                dve.sem_inc(held, 1)
                for t in range(CT):
                    ins = nc.vector.bn_aggr(mv[:, t, :], stats[:, t, :])
                ins.then_inc(s_mv, 1)
                dve.wait_ge(s_mv, q + 1)
                nc.vector.tensor_scalar(veps[:, :], mv[:, :, 1], EPS, None, ALU.add).then_inc(s_veps, 1)

            def apply(q):
                dve.wait_ge(s_rstd, q + 1)
                need(dve, xt_full, q)
                for t in range(CT):
                    ins = nc.vector.tensor_scalar(xn[:, t, :], rows(q, t, 1).rearrange("p o d -> p (o d)"), mv[:, t, 0:1],
                                                  rstd[:, t:t + 1], ALU.subtract, ALU.mult)
                ins.then_inc(s_xn, 1)

            def x_lo(q, k):
                dve.wait_ge(xt_out, 2 * q + 2)
                nc.vector.tensor_tensor(xT_lo[k][:, :], XT[:, :], f32(xT_hi[k][:, :]), ALU.subtract).then_inc(xt_lo, 1)

            def gates(q):
                m = [6 * q]

                def then(ins):
                    m[0] = m[0] + 1
                    ins.then_inc(gate, 1)
                    dve.wait_ge(gate, m[0])

                dve.wait_ge(sc_full, q + 1)
                need(dve, nt_full, q)
                then(nc.vector.tensor_tensor(sc[:, :, :], SC[:, 0:CT * E].rearrange("p (t e) -> p t e", t=CT),
                                             bgb[:, :].rearrange("p (o e) -> p o e", o=1).to_broadcast([P, CT, E]), ALU.add))
                for t in range(CT):
                    mine = sc[:, t, :].rearrange("p (i o) -> p i o", o=1).to_broadcast([P, E, E])
                    other = sc[:, t, :].rearrange("p (o j) -> p o j", o=1).to_broadcast([P, E, E])
                    nc.vector.tensor_tensor(gt[:, t, :, :], other, mine, ALU.is_gt)
                    ins = nc.vector.tensor_tensor(ge[:, t, :, :], other, mine, ALU.is_equal)
                then(ins)
                bf = before[:, :, :].rearrange("p (o i) j -> p o (i j)", o=1).to_broadcast([P, CT, E * E])
                then(nc.vector.tensor_tensor(ge[:, :, :, :].rearrange("p t i j -> p t (i j)"),
                                             ge[:, :, :, :].rearrange("p t i j -> p t (i j)"), bf, ALU.mult))
                then(nc.vector.tensor_tensor(gt[:, :, :, :], gt[:, :, :, :], ge[:, :, :, :], ALU.add))
                then(nc.vector.tensor_reduce(rank[:, :, :], gt[:, :, :, :], mybir.AxisListType.X, ALU.add))
                then(nc.vector.tensor_scalar(unsel[:, :, :], rank[:, :, :], 1.5, None, ALU.is_gt))

            def select(q, k):
                dve.wait_ge(nt_full, q + 1)
                need(dve, y_full, q - 1)
                nc.vector.tensor_copy(unselT[k][:, :], NT[0:E, :])
                nc.vector.tensor_scalar(selT[k][:, :], NT[0:E, :], -1.0, 1.0, ALU.mult, ALU.add).then_inc(seled, 1)

            def low(q, j):
                n = J * q + j
                dve.wait_ge(g_his, n + 1)
                nc.vector.tensor_tensor(g_lo[j % 4][:, :], g[j % 4][:, :], f32(g_hi[j % 4][:, :]),
                                        ALU.subtract).then_inc(g_los, 1)

            def result(q, k):
                dve.wait_ge(ot_full, q + 1)
                need(dve, yo_stored[k], 8 * (q - k))
                nc.vector.tensor_tensor(yo[k][:, :, :], OT[:, :].rearrange("p (t d) -> p t d", t=CT), rows(q, 0, CT),
                                        ALU.add).then_inc(yo_made, 1)

            norm(0)
            apply(0)
            dve.wait_ge(w_raw_in, 32)
            dve.wait_ge(small_in, 48)
            dve.wait_ge(consts, 5)
            nc.vector.tensor_copy(w1_hi[:, :, :], w1_raw[:, :, :])
            nc.vector.tensor_copy(w2_hi[:, :, :], w2_raw[:, :, :])
            nc.vector.tensor_copy(far[:, :, :], far_raw[:, :, :])
            nc.vector.tensor_copy(b2_hi[:, :], b2_raw[:, :]).then_inc(wsplit, 1)
            dve.wait_ge(wsplit, 1)
            nc.vector.tensor_tensor(w1_lo[:, :, :], w1_raw[:, :, :], f32(w1_hi[:, :, :]), ALU.subtract)
            nc.vector.tensor_tensor(w2_lo[:, :, :], w2_raw[:, :, :], f32(w2_hi[:, :, :]), ALU.subtract)
            nc.vector.tensor_tensor(b2_lo[:, :], b2_raw[:, :], f32(b2_hi[:, :]), ALU.subtract).then_inc(wsplit, 1)
            dve.wait_ge(bg_full, 1)
            nc.vector.tensor_copy(bgb[:, :], NT[:, 0:E]).then_inc(wsplit, 1)
            dve.wait_ge(wsplit, 3)
            x_lo(0, 0)
            gates(0)
            select(0, 0)

            def step(q, k):
                for j in range(J):
                    if not last(q):
                        if j == 2:
                            norm(q + 1)
                        if j == 5:
                            apply(q + 1)
                        if j == 9:
                            x_lo(q + 1, 1 - k)
                        if j == 12:
                            gates(q + 1)
                        if j == 15:
                            select(q + 1, 1 - k)
                    low(q, j)
                result(q, k)

            loop(dve, step)

        @block.tensor
        def _(pe):
            def turn(q):
                pe.wait_ge(s_xn, q + 1)
                need(pe, xt_lo, q)
                for t in range(CT):
                    ins = nc.tensor.transpose(XT[:, P * t:P * t + P], xn[:, t, :], ident[:, :])
                ins.then_inc(xt_full, 1)

            def scores(q):
                pe.wait_ge(xt_out, 2 * q + 1)
                need(pe, gate, 6 * (q - 1) + 1)
                for t in range(CT):
                    ins = nc.tensor.matmul(SC[:, E * t:E * t + E], xT[:, P * t:P * t + P], wg[:, :], start=True, stop=True)
                ins.then_inc(sc_full, 1)

            def unselected(q):
                pe.wait_ge(gate, 6 * q + 6)
                need(pe, seled, q)
                for t in range(CT):
                    ins = nc.tensor.transpose(NT[0:E, P * t:P * t + P], unsel[:, t, :], ident[:, :])
                ins.then_inc(nt_full, 1)

            def up(q, k, j):
                n = J * q + j
                need(pe, g_made, n - 1)
                e, c = j // HC, j % HC
                u = U[j % 2]
                for i, (w, r) in enumerate(((w1_hi, xT_hi), (w1_hi, xT_lo), (w1_lo, xT_hi))):
                    nc.tensor.matmul(u[:, :], w[:, e, P * c:P * c + P], r[k][:, :], start=(i == 0), stop=False)
                nc.tensor.matmul(u[:, :], far[:, e, :], unselT[k][:, :], start=False, stop=True).then_inc(u_full, 1)

            def down_product(q, k, j):
                n = J * q + j
                pe.wait_ge(g_los, n + 1)
                if j == 0:
                    need(pe, y_out, q)
                for i, (w, r) in enumerate(((w2_hi, g_hi), (w2_hi, g_lo), (w2_lo, g_hi))):
                    ins = nc.tensor.matmul(Y[:, :], w[:, j, :], r[j % 4][:, :], start=(i == 0 and j == 0), stop=False)
                ins.then_inc(down, 1)

            pe.wait_ge(small_in, 48)
            pe.wait_ge(consts, 1)
            nc.tensor.matmul(NT[:, 0:E], ones[:, :], bg_row[:, :], start=True, stop=True).then_inc(bg_full, 1)
            turn(0)
            scores(0)
            pe.wait_ge(wsplit, 3)
            unselected(0)

            def step(q, k):
                pe.wait_ge(seled, q + 1)
                pe.wait_ge(xt_lo, q + 1)
                for j in range(J + 2):
                    if j < J:
                        up(q, k, j)
                    if j >= 2:
                        down_product(q, k, j - 2)
                    if not last(q):
                        if j == 7:
                            turn(q + 1)
                        if j == 10:
                            scores(q + 1)
                        if j == 14:
                            unselected(q + 1)
                nc.tensor.matmul(Y[:, :], b2_hi[:, :], selT[k][:, :], start=False, stop=False)
                nc.tensor.matmul(Y[:, :], b2_lo[:, :], selT[k][:, :], start=False, stop=True).then_inc(y_full, 1)
                pe.wait_ge(y_out, q + 1)
                need(pe, yo_made, q)
                for t in range(CT):
                    ins = nc.tensor.transpose(OT[:, P * t:P * t + P], yT[:, P * t:P * t + P], ident[:, :])
                ins.then_inc(ot_full, 1)

            loop(pe, step)


_INS = ['x', 'adj', 'L0_gnn_weight', 'L0_gnn_w_ih', 'L0_gnn_w_hh', 'L0_gnn_b_ih', 'L0_gnn_b_hh', 'L0_ffn_Wg',
        'L0_ffn_bg', 'L0_ffn_W1', 'L0_ffn_b1', 'L0_ffn_W2', 'L0_ffn_b2']


def kernel(**inputs):
    import numpy as _np
    import concourse.bacc as _bacc
    from concourse import mybir as _mybir
    from concourse.bass_utils import run_bass_kernel_spmd as _run

    nc = _bacc.Bacc("TRN2", target_bir_lowering=False, num_devices=1)
    arrays, args = {}, []
    for name in _INS:
        a = _np.ascontiguousarray(inputs[name])
        arrays[f"in_{name}_dram"] = a
        args.append(nc.dram_tensor(f"in_{name}_dram", a.shape, _mybir.dt.from_np(a.dtype), kind="ExternalInput").ap())
    args.append(nc.dram_tensor("out_0_dram", (8, 1024, 128), _mybir.dt.float32, kind="ExternalOutput").ap())
    gnn_ffn(nc, *args)
    r = _run(nc, [arrays], core_ids=[0])
    return r.results[0]["out_0_dram"]
```

```python
import concourse.bass as bass
from concourse import mybir
from contextlib import ExitStack

F32 = mybir.dt.float32
R32 = mybir.dt.float32r
I32 = mybir.dt.int32
U32 = mybir.dt.uint32
BF16 = mybir.dt.bfloat16
ALU = mybir.AluOpType
ACT = mybir.ActivationFunctionType

P = 128
B = 8
N = 1024
T = N // P
LAYERS = 3
CH = 512
CT = CH // P
EPS = 1e-5
STG = 4


def f32(ap):
    return ap.bitcast(F32)


def need(eng, sem, value):
    if isinstance(value, int) and value <= 0:
        return
    eng.wait_ge(sem, value)


E = 8
HC = 2
J = E * HC
TOP = 2
ROUND_GRAPHS = (5, 3)
ROUNDS = len(ROUND_GRAPHS)
FIRST_GRAPH = [sum(ROUND_GRAPHS[:r]) for r in range(ROUNDS + 1)]
REG = max(ROUND_GRAPHS) * N + CH
TILES = [n * N * TOP // CH + E for n in ROUND_GRAPHS]
FIRST_TILE = [sum(TILES[:r]) for r in range(ROUNDS + 1)]
SPARE = E * REG
RS = SPARE + max(TILES) * CH


def round_of(b):
    return 0 if not isinstance(b, int) or b < FIRST_GRAPH[1] else 1


def gnn_ffn(nc, x, adj, weight, w_ih, w_hh, b_ih, b_hh, Wg, bg, W1, b1, W2, b2, out):
    with ExitStack() as whole:
        def sb(name, shape, dt=F32):
            return whole.enter_context(nc.sbuf_tensor(name, shape, dt))

        def sem(name):
            return whole.enter_context(nc.semaphore(name))

        bank = [whole.enter_context(nc.psum_tensor(f"bank{i}", [P, CH], F32)) for i in range(8)]
        x2 = sb("x2", [P, B * T, P])
        ident = sb("ident", [P, P])
        sorted_x = [nc.dram_tensor(f"sorted_x{r}", (RS, P), F32, kind="Internal").ap() for r in range(ROUNDS)]
        sorted_y = [nc.dram_tensor(f"sorted_y{r}", (TILES[r] * CH, P), F32, kind="Internal").ap() for r in range(ROUNDS)]
        route = Routing(nc, sb, sem, x2, ident, sorted_x)
        graphs(nc, x, adj, weight, w_ih, w_hh, b_ih, b_hh, Wg, bg, bank, x2, ident, route, sem)
        experts(nc, W1, b1, W2, b2, out, bank, x2, ident, sorted_x, sorted_y, route, sem)


class Routing:

    LAST = 12 * B - 6

    def __init__(self, nc, sb, sem, x2, ident, sorted_x):
        self.nc, self.x2, self.ident, self.sorted_x = nc, x2, ident, sorted_x
        self.h_last = sb("hT1", [P, 2, CH])
        self.xr = [sb(f"xr{i}", [P, T, P]) for i in range(2)]
        self.xrT = sb("xrT", [P, 2, CH])
        self.st = sb("r_st", [P, T, 6])
        self.mean_var = sb("r_mean_var", [P, T, 2])
        self.veps = sb("r_veps", [P, T])
        self.rstd = sb("r_rstd", [P, T])
        self.shift = sb("r_shift", [P, T])
        self.mhalf = sb("mhalf", [P, T])
        self.wg = sb("wg", [P, E])
        self.bgb = sb("bgb", [P, E])
        self.ones = sb("ones", [P, P], BF16)
        self.earlier = sb("earlier", [P, P], BF16)
        self.sc = sb("sc", [P, T, E])
        self.beats = sb("beats", [P, T, E, E], BF16)
        self.ties = sb("ties", [P, T, E, E], BF16)
        self.before = sb("before", [P, E, E], BF16)
        self.rank = sb("rank", [P, T, E])
        self.sel = sb("sel", [P, T, E])
        self.sel_bf = sb("sel_bf", [P, T + 1, E], BF16)
        self.offset = sb("offset", [P, E])
        self.pos = sb("pos", [P, T, E])
        self.region = sb("region", [P, T, E])
        self.keep_count = sb("keep_count", [P, B])
        self.high_row = sb("high_row", [P, T])
        self.both_rows = sb("both_rows", [P, T])
        self.rows_now = sb("rows_now", [P, T, TOP], I32)
        self.slots = sb("slots", [P, B * T * TOP], I32)
        self.counts = sb("counts", [P, B, E])
        self.pool_passed = sem("pool_passed")
        self.dve_passed = sem("dve_passed")
        self.h_done = sem("h_done")
        self.tr_full = sem("tr_full")
        self.tr_free = sem("tr_free")
        self.r_stats = sem("r_stats")
        self.r_mv = sem("r_mv")
        self.r_scale_in = sem("r_scale_in")
        self.r_scale = sem("r_scale")
        self.r_xr = sem("r_xr")
        self.gate = sem("gate")
        self.placed = sem("placed")
        self.rows_made = sem("rows_made")
        self.scattered = sem("scattered")

    def tile(self, b, t, n=1):
        at = T * b + t
        v = self.x2[:, at:at + n, :] if isinstance(at, int) else self.x2[:, bass.ds(at, n), :]
        return v.rearrange("p o d -> p (o d)") if n == 1 else v

    def per_graph(self, v, b, n=1):
        return v[:, n * b:n * b + n] if isinstance(b, int) else v[:, bass.ds(n * b, n)]


    def output_turn(self, pe, n, c, bank, tr, alone=False):
        pe.wait_ge(self.h_done, n + 1)
        need(pe, self.tr_free, tr if alone else tr - 1)
        for t in range(CT):
            ins = self.nc.tensor.transpose(bank[:, P * t:P * t + P], self.h_last[:, c, P * t:P * t + P], self.ident[:, :])
        ins.then_inc(self.tr_full, 1)

    def result_turn(self, pe, b, half, c, bank, tr, alone=False):
        pe.wait_ge(self.r_xr, b + 1)
        pe.wait_ge(self.tr_free, tr if alone else tr - 1)
        for t in range(CT):
            ins = self.nc.tensor.transpose(bank[:, P * t:P * t + P], self.xr[half][:, CT * c + t, :], self.ident[:, :])
        ins.then_inc(self.tr_full, 1)

    def scores(self, pe, b, bank, tr, alone=False):
        pe.wait_ge(self.tr_free, tr if alone else tr - 1)
        for t in range(T):
            ins = self.nc.tensor.matmul(bank[:, E * t:E * t + E], self.xrT[:, t // CT, P * (t % CT):P * (t % CT) + P],
                                        self.wg[:, :], start=True, stop=True)
        ins.then_inc(self.tr_full, 1)

    def count(self, pe, b, bank, tr, alone=False):
        pe.wait_ge(self.gate, 7 * b + 6)
        pe.wait_ge(self.tr_free, tr if alone else tr - 1)
        self.nc.tensor.matmul(bank[:, 0:T * E + E], self.earlier[:, :], self.sel_bf[:, :, :].rearrange("p t e -> p (t e)"),
                              start=True, stop=False)
        for t in range(T):
            n = T - t
            ins = self.nc.tensor.matmul(bank[:, E * t + E:T * E + E], self.ones[:, :],
                                        self.sel_bf[:, t:t + 1, :].to_broadcast([P, n, E]),
                                        start=False, stop=(t == T - 1))
        ins.then_inc(self.tr_full, 1)


    def scale(self, pool, b):
        pool.wait_ge(self.r_scale_in, b + 1)
        self.nc.gpsimd.tensor_tensor(self.rstd[:, :], self.veps[:, :], self.mhalf[:, :], ALU.pow).then_inc(self.r_scale, 1)
        pool.wait_ge(self.r_scale, 2 * b + 1)
        self.nc.gpsimd.tensor_tensor(self.shift[:, :], self.shift[:, :], self.rstd[:, :], ALU.mult).then_inc(self.r_scale, 1)

    def scatter(self, pool, b, half, first, end):
        pool.wait_ge(self.rows_made, b + 1)
        pool.sem_inc(self.pool_passed, 1)
        for t in range(first, end):
            for k in range(TOP):
                self.nc.gpsimd.indirect_dma_start(
                    out=self.sorted_x[round_of(b)],
                    out_offset=bass.IndirectOffsetOnAxis(ap=self.rows_now[:, t, k:k + 1].bitcast(U32), axis=0),
                    in_=self.xr[half][:, t, :], in_offset=None).then_inc(self.scattered, 16)


    def normalise(self, b, dst, rs, sh, done):
        for t in range(T):
            ins = self.nc.scalar.activation(dst[:, t, :], self.tile(b, t), ACT.Identity, bias=sh[:, t:t + 1], scale=rs[:, t:t + 1])
        ins.then_inc(done, 1)

    def apply(self, act, b, half):
        act.wait_ge(self.r_scale, 2 * b + 2)
        need(act, self.scattered, 16 * TOP * T * (b - 1))
        self.normalise(b, self.xr[half], self.rstd, self.shift, self.r_xr)

    def turned(self, act, b, c, bank, tr):
        act.wait_ge(self.tr_full, tr + 1)
        need(act, self.gate, 7 * (b - 1) + 1)
        self.nc.scalar.activation(self.xrT[:, c, :], bank[:, :], ACT.Copy).then_inc(self.tr_free, 1)


    def moments(self, dve, b, st, m, ve, sh, s_stats, s_mv, s_veps):
        nc = self.nc
        dve.sem_inc(self.dve_passed, 1)
        for t in range(T):
            ins = nc.vector.bn_stats(st[:, t, :], self.tile(b, t))
        ins.then_inc(s_stats, 1)
        dve.wait_ge(s_stats, b + 1)
        dve.sem_inc(self.dve_passed, 1)
        for t in range(T):
            ins = nc.vector.bn_aggr(m[:, t, :], st[:, t, :])
        ins.then_inc(s_mv, 1)
        dve.wait_ge(s_mv, b + 1)
        nc.vector.tensor_scalar(sh[:, :], m[:, :, 0], -1.0, None, ALU.mult)
        nc.vector.tensor_scalar(ve[:, :], m[:, :, 1], EPS, None, ALU.add).then_inc(s_veps, 1)

    def residual(self, dve, b, c, bank, tr):
        dve.wait_ge(self.tr_full, tr + 1)
        self.nc.vector.tensor_tensor(self.tile(b, CT * c, CT), bank[:, :].rearrange("p (t d) -> p t d", t=CT),
                                     self.tile(b, CT * c, CT), ALU.add).then_inc(self.tr_free, 1)

    def norm(self, dve, b, tr):
        dve.wait_ge(self.tr_free, tr + 1)
        need(dve, self.r_xr, b)
        self.moments(dve, b, self.st, self.mean_var, self.veps, self.shift, self.r_stats, self.r_mv, self.r_scale_in)

    def gates(self, dve, b, bank, tr):
        nc = self.nc
        m = 7 * b
        beats, ties, rank = self.beats, self.ties, self.rank
        dve.wait_ge(self.tr_full, tr + 1)
        nc.vector.tensor_tensor(self.sc[:, :, :], bank[:, 0:T * E].rearrange("p (t e) -> p t e", t=T),
                                self.bgb[:, :].rearrange("p (o e) -> p o e", o=1).to_broadcast([P, T, E]),
                                ALU.add).then_inc(self.tr_free, 1)
        dve.wait_ge(self.tr_free, tr + 1)
        mine = self.sc[:, :, :].rearrange("p t (i o) -> p t i o", o=1).to_broadcast([P, T, E, E])
        other = self.sc[:, :, :].rearrange("p t (o j) -> p t o j", o=1).to_broadcast([P, T, E, E])
        nc.vector.tensor_tensor(ties[:, :, :, :], other, mine, ALU.is_equal).then_inc(self.gate, 1)
        nc.vector.tensor_tensor(beats[:, :, :, :], other, mine, ALU.is_gt).then_inc(self.gate, 1)
        lower = self.before[:, :, :].rearrange("p (o i) j -> p o (i j)", o=1).to_broadcast([P, T, E * E])
        flat = ties[:, :, :, :].rearrange("p t i j -> p t (i j)")
        dve.wait_ge(self.gate, m + 1)
        nc.vector.tensor_tensor(flat, flat, lower, ALU.mult).then_inc(self.gate, 1)
        dve.wait_ge(self.gate, m + 3)
        nc.vector.tensor_tensor(beats[:, :, :, :], beats[:, :, :, :], ties[:, :, :, :], ALU.add).then_inc(self.gate, 1)
        dve.wait_ge(self.gate, m + 4)
        nc.vector.tensor_reduce(rank[:, :, :], beats[:, :, :, :], mybir.AxisListType.X, ALU.add).then_inc(self.gate, 1)
        dve.wait_ge(self.gate, m + 5)
        nc.vector.tensor_scalar(self.sel_bf[:, 0:T, :], rank[:, :, :], TOP - 0.5, None, ALU.is_lt).then_inc(self.gate, 1)
        nc.vector.tensor_scalar(self.sel[:, :, :], rank[:, :, :], TOP - 0.5, None, ALU.is_lt).then_inc(self.gate, 1)

    def places(self, dve, b, bank, tr):
        nc = self.nc
        m = 8 * b
        pos = self.pos
        nc.vector.tensor_scalar(self.offset[:, :], self.offset[:, :], self.per_graph(self.keep_count, b), None,
                                ALU.mult).then_inc(self.placed, 1)
        dve.wait_ge(self.placed, m + 1)
        dve.wait_ge(self.tr_full, tr + 1)
        so_far = self.offset[:, :].rearrange("p (o e) -> p o e", o=1).to_broadcast([P, T, E])
        nc.vector.tensor_tensor(pos[:, :, :], bank[:, 0:T * E].rearrange("p (t e) -> p t e", t=T), so_far,
                                ALU.add).then_inc(self.placed, 1)
        nc.vector.tensor_tensor(self.per_graph(self.counts[:, :, :].rearrange("p b e -> p (b e)"), b, E),
                                bank[:, T * E:T * E + E], self.offset[:, :], ALU.add).then_inc(self.placed, 1)
        dve.wait_ge(self.placed, m + 2)
        nc.vector.tensor_tensor(pos[:, :, :], pos[:, :, :], self.region[:, :, :], ALU.add).then_inc(self.placed, 1)
        dve.wait_ge(self.placed, m + 3)
        nc.vector.tensor_tensor(self.offset[:, :], bank[:, T * E:T * E + E], self.offset[:, :], ALU.add).then_inc(self.tr_free, 1)
        dve.wait_ge(self.placed, m + 4)
        dve.wait_ge(self.gate, 7 * b + 7)
        nc.vector.tensor_tensor(pos[:, :, :], pos[:, :, :], self.sel[:, :, :], ALU.mult).then_inc(self.placed, 1)
        dve.wait_ge(self.placed, m + 5)
        nc.vector.tensor_reduce(self.high_row[:, :], pos[:, :, :], mybir.AxisListType.X, ALU.max)
        nc.vector.tensor_reduce(self.both_rows[:, :], pos[:, :, :], mybir.AxisListType.X, ALU.add).then_inc(self.placed, 1)
        dve.wait_ge(self.placed, m + 6)
        need(dve, self.scattered, 16 * TOP * T * b)
        nc.vector.scalar_tensor_tensor(out=self.rows_now[:, :, 0], in0=self.both_rows[:, :], scalar=-1.0, in1=self.high_row[:, :],
                                       op0=ALU.add, op1=ALU.subtract)
        nc.vector.tensor_scalar(self.rows_now[:, :, 1], self.high_row[:, :], -1.0, None, ALU.add).then_inc(self.placed, 1)
        dve.wait_ge(self.placed, m + 7)
        nc.vector.tensor_copy(self.per_graph(self.slots, b, T * TOP),
                              self.rows_now[:, :, :].rearrange("p t k -> p (t k)")).then_inc(self.placed, 1)
        dve.wait_ge(self.placed, m + 8)
        dve.wait_ge(self.tr_free, tr + 1)
        dve.sem_inc(self.rows_made, 1)
def graphs(nc, x, adj, weight, w_ih, w_hh, b_ih, b_hh, Wg, bg, bank, x2, ident, route, sem):
    with ExitStack() as ctx:
        def sb(name, shape, dt=F32):
            return ctx.enter_context(nc.sbuf_tensor(name, shape, dt))

        AG = bank[0:2]
        R, Z, HN, IN = bank[2:6]
        TR = bank[6:8]
        stage = sb("stage", [P, STG, N], I32)
        A = [sb(f"A{i}", [P, T, N], R32) for i in range(2)]
        hT = [sb("hT0", [P, 2, CH]), route.h_last]
        hT_hi = [sb(f"hT_hi{i}", [P, 2, CH], R32) for i in range(2)]
        hT_lo = [sb(f"hT_lo{i}", [P, 2, CH], R32) for i in range(2)]
        hN_hi = [sb(f"hN_hi{i}", [P, T, P], R32) for i in range(2)]
        hN_lo = [sb(f"hN_lo{i}", [P, T, P], R32) for i in range(2)]
        ag_hi = [sb(f"ag_hi{i}", [P, CH], R32) for i in range(2)]
        ag_lo = [sb(f"ag_lo{i}", [P, CH], R32) for i in range(2)]
        rt = [sb(f"rt{i}", [P, CH]) for i in range(2)]
        zt = [sb(f"zt{i}", [P, CH]) for i in range(2)]
        zh = [sb(f"zh{i}", [P, CH]) for i in range(2)]
        xn = sb("xn", [P, T, P])
        stats = sb("stats", [P, T, 6])
        mv = sb("mv", [P, T, 2])
        veps = sb("veps", [P, T])
        rstd = sb("rstd", [P, T])
        shift = sb("shift", [P, T])
        wi_hi = sb("wi_hi", [P, LAYERS, 3, P], R32)
        wi_lo = sb("wi_lo", [P, LAYERS, 3, P], R32)
        wh_hi = sb("wh_hi", [P, 3, P], R32)
        wh_lo = sb("wh_lo", [P, 3, P], R32)
        bcol = sb("bcol", [P, 6])
        brz = sb("brz", [P, 2])
        wg = route.wg
        bgb = route.bgb
        bg_row = sb("bg_row", [1, E])
        ones_row = sb("ones_row", [1, P])
        w_raw = rt[0][:, 0:384].rearrange("p (i e) -> p i e", i=3)
        wih_raw = rt[1][:, 0:384].rearrange("p (i e) -> p i e", i=3)
        whh_raw = zt[0][:, 0:384].rearrange("p (i e) -> p i e", i=3)
        wT = zt[1][:, 0:384].rearrange("p (i e) -> p i e", i=3)
        wihT = zh[0][:, 0:384]
        brow = zh[1][0:6, 0:P]

        id_made = sem("id_made")
        h_done, tr_full, tr_free, scattered, r_xr, gate = route.h_done, route.tr_full, route.tr_free, route.scattered, route.r_xr, route.gate

        w_loaded = sem("w_loaded")
        w_turned = sem("w_turned")
        w_taken = sem("w_taken")
        w_fused = sem("w_fused")
        w_split = sem("w_split")
        stage_in = [sem(f"stage_in{i}") for i in range(STG)]
        a_made = sem("a_made")
        x_in = sem("x_in")
        ln_stats = sem("ln_stats")
        ln_mv = sem("ln_mv")
        ln_veps = sem("ln_veps")
        ln_rstd = sem("ln_rstd")
        ln_xn = sem("ln_xn")
        prep_hi = sem("prep_hi")
        prep_lo = sem("prep_lo")
        prep_t = sem("prep_t")
        bg_full = sem("bg_full")
        tok_hi = sem("tok_hi")
        ag_full = sem("ag_full")
        ag_his = sem("ag_his")
        ag_los = sem("ag_los")
        r_full = sem("r_full")
        z_full = sem("z_full")
        hn_full = sem("hn_full")
        in_full = sem("in_full")
        r_done = sem("r_done")
        z_done = sem("z_done")
        t_done = sem("t_done")
        t2_done = sem("t2_done")
        n_done = sem("n_done")
        v_done = sem("v_done")
        zh_done = sem("zh_done")
        hhi_done = sem("hhi_done")
        hlo_done = sem("hlo_done")

        def chunk_no(it, half, l, c):
            return 12 * it + 6 * half + 2 * l + c

        def tr_no(it, half, k):
            if is_first(it, half):
                return k if k < 6 else k - 2
            if is_last(it, half) and k >= 10:
                k -= 2
            return 24 * it + 12 * half - 4 + k

        def loop(eng, pair):
            pair(0)
            with eng.Fori(1, B // 2 - 1) as it:
                pair(it)
            pair(B // 2 - 1)

        def is_last(it, half):
            return half == 1 and isinstance(it, int) and it == B // 2 - 1

        def prev(it, half):
            return (it, 0) if half else (it - 1, 1)

        def routed(it, half):
            return not (isinstance(it, int) and it == 0)

        def is_first(it, half):
            return half == 0 and isinstance(it, int) and it == 0

        def hidden(l, what, half=None):
            return what[0] if l == 0 else what[1]

        block = ctx.enter_context(nc.Block())

        @block.sync
        def _(sp):
            av = adj.rearrange("b (t p) n -> b t p n", p=P)

            def rows(b, t, n):
                need(sp, a_made, n - STG + 1)
                sp.dma_start(stage[:, t % STG, :], av[b, t, :, :] if isinstance(b, int)
                             else av[bass.ds(b, 1), t, :, :].rearrange("o p n -> (o p) n")).then_inc(stage_in[t % STG], 16)

            for t in range(T):
                rows(0, t, t)

            sp.dma_start(x2[:, T:B * T, :], x.rearrange("b (t p) d -> p (b t) d", p=P)[:, T:B * T, :]).then_inc(x_in, 16)

            def pair(it):
                for half in range(2):
                    if not is_last(it, half):
                        nxt = 2 * it + half + 1
                        for t in range(T):
                            rows(nxt, t, 8 * nxt + t)

            loop(sp, pair)

        @block.gpsimd
        def _(pool):
            nc.gpsimd.memset(route.mhalf[:, :], -0.5).then_inc(id_made, 1)
            nc.gpsimd.memset(ident[:, :], 0.0).then_inc(id_made, 1)
            pool.wait_ge(id_made, 2)
            nc.gpsimd.affine_select(out=ident[:, :], in_=ident[:, :], compare_op=ALU.not_equal, fill=1.0,
                                    base=0, pattern=[[-1, P]], channel_multiplier=1).then_inc(id_made, 1)

            nc.gpsimd.memset(ones_row[:, :], 1.0).then_inc(id_made, 1)
            nc.gpsimd.memset(route.ones[:, :], 1.0).then_inc(id_made, 1)
            nc.gpsimd.memset(route.earlier[:, :], 1.0).then_inc(id_made, 1)
            nc.gpsimd.memset(route.before[:, :, :], 1.0).then_inc(id_made, 1)
            nc.gpsimd.memset(route.offset[:, :], 0.0).then_inc(id_made, 1)
            nc.gpsimd.memset(route.keep_count[:, :], 1.0).then_inc(id_made, 1)
            pool.wait_ge(id_made, 9)
            nc.gpsimd.affine_select(out=route.earlier[:, :], in_=route.earlier[:, :], compare_op=ALU.is_gt, fill=0.0,
                                    base=0, pattern=[[1, P]], channel_multiplier=-1).then_inc(id_made, 1)
            nc.gpsimd.affine_select(out=route.before[:, :, :], in_=route.before[:, :, :], compare_op=ALU.is_gt, fill=0.0,
                                    base=0, pattern=[[1, E], [-1, E]], channel_multiplier=0).then_inc(id_made, 1)
            for e in range(E):
                ins = nc.gpsimd.memset(route.region[:, :, e], float(e * REG + 1))
            for r in range(ROUNDS):
                ins = nc.gpsimd.memset(route.keep_count[:, FIRST_GRAPH[r]:FIRST_GRAPH[r] + 1], 0.0)
            nc.gpsimd.memset(route.sel_bf[:, T, :], 0.0)
            ins.then_inc(id_made, 1)

            def input_scale(nb):
                pool.wait_ge(ln_veps, nb + 1)
                nc.gpsimd.tensor_tensor(rstd[:, :], veps[:, :], route.mhalf[:, :], ALU.pow).then_inc(ln_rstd, 1)
                pool.wait_ge(ln_rstd, 2 * nb + 1)
                nc.gpsimd.tensor_tensor(shift[:, :], shift[:, :], rstd[:, :], ALU.mult).then_inc(ln_rstd, 1)

            def input_lo(nb):
                pool.wait_ge(prep_hi, nb + 1)
                need(pool, ag_full, 6 * (nb - 1) + 2)
                nc.gpsimd.tensor_tensor(hN_lo[0][:, :, :], xn[:, :, :], f32(hN_hi[0][:, :, :]),
                                        ALU.subtract).then_inc(prep_lo, 1)

            input_scale(0)
            input_lo(0)
            def keep(it, half, l, c):
                n = chunk_no(it, half, l, c)
                pool.wait_ge(z_done, n + 1)
                if l == 0:
                    pool.wait_ge(prep_t, 4 * (2 * it + half) + 4)
                else:
                    pool.wait_ge(h_done, n - 1)
                need(pool, h_done, n - 1)
                nc.gpsimd.tensor_tensor(zh[c][:, :], zt[c][:, :], hidden(l, hT)[:, c, :],
                                        ALU.mult).then_inc(zh_done, 1)

            def pair(it):
                for half in range(2):
                    more = not is_last(it, half)
                    nb = 2 * it + half + 1
                    for l in range(LAYERS):
                        for c in range(2):
                            keep(it, half, l, c)
                        if l == 1 and more:
                            input_scale(nb)
                        if l == 2 and more:
                            input_lo(nb)
                        if routed(it, half):
                            route.scatter(pool, 2 * it + half - 2, half, 3 * l, min(3 * l + 3, T))
                        if l == 0 and not is_first(it, half):
                            route.scale(pool, 2 * it + half - 1)

            loop(pool, pair)

        @block.scalar
        def _(act):
            act.dma_start(x2[:, 0:T, :], x.rearrange("b (t p) d -> b p t d", p=P)[0, :, :, :]).then_inc(x_in, 16)
            act.dma_start(w_raw, weight.rearrange("i d e -> d i e")).then_inc(w_loaded, 16)
            act.dma_start(wih_raw, w_ih.rearrange("(i j) e -> j i e", j=P)).then_inc(w_loaded, 16)
            act.dma_start(whh_raw, w_hh.rearrange("(i j) e -> j i e", j=P)).then_inc(w_loaded, 16)
            act.dma_start(brow[0:3, :], b_ih.rearrange("(i j) -> i j", j=P)).then_inc(w_loaded, 16)
            act.dma_start(brow[3:6, :], b_hh.rearrange("(i j) -> i j", j=P)).then_inc(w_loaded, 16)
            act.dma_start(wg[:, :], Wg).then_inc(w_loaded, 16)
            act.dma_start(bg_row[:, :], bg.rearrange("(o e) -> o e", o=1)).then_inc(w_loaded, 16)

            def input_hi(nb):
                act.wait_ge(ln_xn, nb + 1)
                need(act, ag_full, 6 * (nb - 1) + 2)
                nc.scalar.activation(hN_hi[0][:, :, :], xn[:, :, :], ACT.Copy).then_inc(prep_hi, 1)

            def input_turned(nb, c, tr, k):
                act.wait_ge(tr_full, tr + 1)
                need(act, zh_done, 6 * (nb - 1) + c + 1)
                need(act, hn_full, 6 * (nb - 1) + c + 1)
                nc.scalar.activation(hT[0][:, c, :], TR[k % 2][:, :], ACT.Copy).then_inc(prep_t, 1)
                nc.scalar.activation(hT_hi[0][:, c, :], TR[k % 2][:, :], ACT.Copy).then_inc(prep_t, 1)

            def input_apply(nb):
                act.wait_ge(ln_rstd, 2 * nb + 2)
                need(act, prep_lo, nb)
                need(act, tr_full, (0, 2, 8)[nb] if isinstance(nb, int) and nb < 3 else 12 * nb - 18)
                route.normalise(nb, xn, rstd, shift, ln_xn)

            input_apply(0)
            input_hi(0)
            for c in range(2):
                input_turned(0, c, c, c)

            def node_major_hi(it, half, l, c):
                n = chunk_no(it, half, l, c)
                k = 2 + 2 * l + c
                act.wait_ge(tr_full, tr_no(it, half, k) + 1)
                if c == 0:
                    act.wait_ge(ag_full, n + 2)
                nc.scalar.activation(hN_hi[1][:, CT * c:CT * c + CT, :], TR[k % 2][:, :].rearrange("p (t d) -> p t d", t=CT),
                                     ACT.Copy).then_inc(tok_hi, 1)

            def pair(it):
                for half in range(2):
                    more = not is_last(it, half)
                    nb = 2 * it + half + 1
                    for l in range(LAYERS):
                        for c in range(2):
                            n = chunk_no(it, half, l, c)
                            act.wait_ge(ag_full, n + 1)
                            need(act, in_full, n - 1)
                            nc.scalar.activation(ag_hi[c][:, :], AG[c][:, :], ACT.Copy).then_inc(ag_his, 1)
                            if l == 2 and c == 0 and not is_first(it, half):
                                for k in range(2):
                                    route.turned(act, nb - 2, k, TR[k], tr_no(it, half, 6 + k))
                        for c in range(2):
                            n = chunk_no(it, half, l, c)
                            act.wait_ge(r_full, n + 1)
                            need(act, h_done, n - 1)
                            if is_first(it, half) and l == 0:
                                act.wait_ge(w_split, 4)
                            nc.scalar.activation(rt[c][:, :], R[:, :], ACT.Sigmoid, bias=brz[:, 0:1]).then_inc(r_done, 1)
                            act.wait_ge(z_full, n + 1)
                            nc.scalar.activation(zt[c][:, :], Z[:, :], ACT.Sigmoid, bias=brz[:, 1:2]).then_inc(z_done, 1)
                            if l == 2 and more:
                                input_turned(nb, c, tr_no(it, half, 8 + c), 8 + c)
                            if c == 1 and l < 2:
                                node_major_hi(it, half, l, 0)
                            act.wait_ge(t2_done, n + 1)
                            nc.scalar.activation(rt[c][:, :], rt[c][:, :], ACT.Tanh, bias=bcol[:, 2:3]).then_inc(n_done, 1)
                        if l == 1 and not is_first(it, half):
                            route.apply(act, nb - 2, 1 - half)
                        if l < 2:
                            node_major_hi(it, half, l, 1)
                        if l == 1 and more:
                            input_apply(nb)
                        if l == 2 and more:
                            input_hi(nb)

            loop(act, pair)
        @block.vector
        def _(dve):
            def input_norm(nb):
                dve.wait_ge(x_in, 16 if isinstance(nb, int) and nb == 0 else 32)
                need(dve, ln_xn, nb)
                route.moments(dve, nb, stats, mv, veps, shift, ln_stats, ln_mv, ln_veps)

            def convert(half, t, nb):
                dve.wait_ge(stage_in[t % STG], 16 * (2 * nb + t // STG + 1))
                if t == 0:
                    need(dve, ag_full, 6 * (nb - 1))
                nc.vector.tensor_scalar(A[half][:, t, :], stage[:, t % STG, :], 0, None,
                                        ALU.not_equal).then_inc(a_made, 1)

            def input_turned_lo(nb, c, k):
                dve.wait_ge(prep_t, 4 * nb + 2 * c + 2)
                need(dve, hn_full, 6 * (nb - 1) + c + 1)
                nc.vector.tensor_tensor(hT_lo[0][:, c, :], TR[k % 2][:, :], f32(hT_hi[0][:, c, :]),
                                        ALU.subtract).then_inc(tr_free, 1)

            input_norm(0)
            dve.wait_ge(w_turned, 4)
            nc.vector.tensor_copy(wT, AG[0][:, 0:384].rearrange("p (i e) -> p i e", i=3)).then_inc(w_taken, 1)
            nc.vector.tensor_copy(wihT, AG[1][:, 0:384]).then_inc(w_taken, 1)
            nc.vector.tensor_copy(bcol[:, :], Z[:, 0:6]).then_inc(w_taken, 1)
            nc.vector.tensor_copy(wh_hi[:, :, :], R[:, 0:384].rearrange("p (i e) -> p i e", i=3)).then_inc(w_taken, 1)
            dve.wait_ge(w_taken, 4)
            nc.vector.tensor_tensor(brz[:, :], bcol[:, 0:2], bcol[:, 3:5], ALU.add).then_inc(w_split, 1)
            nc.vector.tensor_tensor(wh_lo[:, :, :], R[:, 0:384].rearrange("p (i e) -> p i e", i=3),
                                    f32(wh_hi[:, :, :]), ALU.subtract).then_inc(w_split, 1)
            dve.wait_ge(bg_full, 1)
            nc.vector.tensor_copy(bgb[:, :], TR[0][:, 0:E]).then_inc(w_taken, 1)
            fused = [HN, IN, AG[0]]
            dve.wait_ge(w_fused, 1)
            for l in range(LAYERS):
                src = fused[l][:, 0:384].rearrange("p (i e) -> p i e", i=3)
                ins = nc.vector.tensor_copy(wi_hi[:, l, :, :], src)
            ins.then_inc(w_split, 1)
            dve.wait_ge(w_split, 3)
            for l in range(LAYERS):
                src = fused[l][:, 0:384].rearrange("p (i e) -> p i e", i=3)
                ins = nc.vector.tensor_tensor(wi_lo[:, l, :, :], src, f32(wi_hi[:, l, :, :]), ALU.subtract)
            ins.then_inc(w_split, 1)
            for c in range(2):
                input_turned_lo(0, c, c)
            for t in range(T):
                convert(0, t, 0)

            def node_major_lo(it, half, l, c):
                n = chunk_no(it, half, l, c)
                k = 2 + 2 * l + c
                dve.wait_ge(tok_hi, 8 * it + 4 * half + 2 * l + c + 1)
                nc.vector.tensor_tensor(hN_lo[1][:, CT * c:CT * c + CT, :], TR[k % 2][:, :].rearrange("p (t d) -> p t d", t=CT),
                                        f32(hN_hi[1][:, CT * c:CT * c + CT, :]), ALU.subtract).then_inc(tr_free, 1)

            def converts(half, nb, more, *tiles):
                if more:
                    for t in tiles:
                        convert((half + 1) % 2, t, nb)

            def pair(it):
                for half in range(2):
                    more = not is_last(it, half)
                    nb = 2 * it + half + 1
                    for l in range(LAYERS):
                        if l == 0 and routed(it, half):
                            route.places(dve, nb - 3, TR[1], tr_no(*prev(it, half), 11))
                        if l == 0 and not is_first(it, half):
                            for c in range(2):
                                route.residual(dve, nb - 2, c, TR[c], tr_no(it, half, c))
                        for c in range(2):
                            n = chunk_no(it, half, l, c)
                            dve.wait_ge(ag_his, n + 1)
                            nc.vector.tensor_tensor(ag_lo[c][:, :], AG[c][:, :], f32(ag_hi[c][:, :]),
                                                    ALU.subtract).then_inc(ag_los, 1)
                        if l == 2:
                            converts(half, nb, more, 6)
                        for c in range(2):
                            n = chunk_no(it, half, l, c)
                            dve.wait_ge(r_done, n + 1)
                            dve.wait_ge(hn_full, n + 1)
                            nc.vector.scalar_tensor_tensor(out=rt[c][:, :], in0=HN[:, :], scalar=bcol[:, 5:6],
                                                           in1=rt[c][:, :], op0=ALU.add, op1=ALU.mult).then_inc(t_done, 1)
                            dve.wait_ge(t_done, n + 1)
                            dve.wait_ge(in_full, n + 1)
                            nc.vector.tensor_tensor(rt[c][:, :], IN[:, :], rt[c][:, :], ALU.add).then_inc(t2_done, 1)
                            if c == 1 and l < 2:
                                node_major_lo(it, half, l, 0)
                            if l == 2 and more:
                                input_turned_lo(nb, c, c)
                            if l == 0 and c == 0:
                                converts(half, nb, more, 0)
                            if l == 1 and c == 0 and more:
                                input_norm(nb)
                            dve.wait_ge(n_done, n + 1)
                            dve.wait_ge(z_done, n + 1)
                            nc.vector.scalar_tensor_tensor(out=rt[c][:, :], in0=zt[c][:, :], scalar=1.0, in1=rt[c][:, :],
                                                           op0=ALU.subtract, op1=ALU.mult).then_inc(v_done, 1)
                            dve.wait_ge(v_done, n + 1)
                            dve.wait_ge(zh_done, n + 1)
                            nc.vector.tensor_tensor(hT[1][:, c, :], zh[c][:, :], rt[c][:, :],
                                                    ALU.subtract).then_inc(h_done, 1)
                            if l < 2:
                                dve.wait_ge(h_done, n + 1)
                                nc.vector.tensor_copy(hT_hi[1][:, c, :], hT[1][:, c, :]).then_inc(hhi_done, 1)
                                dve.wait_ge(hhi_done, 8 * it + 4 * half + 2 * l + c + 1)
                                nc.vector.tensor_tensor(hT_lo[1][:, c, :], hT[1][:, c, :], f32(hT_hi[1][:, c, :]),
                                                        ALU.subtract).then_inc(hlo_done, 1)
                            if l == 2 and c == 0:
                                converts(half, nb, more, 7)
                        if l < 2:
                            node_major_lo(it, half, l, 1)
                        if l == 0 and not is_first(it, half):
                            route.norm(dve, nb - 2, tr_no(it, half, 1))
                        if l < 2:
                            converts(half, nb, more, *((1,), (2, 3, 4, 5))[l])
                        if l == 2 and not is_first(it, half):
                            route.gates(dve, nb - 2, TR[0], tr_no(it, half, 10))

            loop(dve, pair)
        @block.tensor
        def _(pe):
            pe.wait_ge(id_made, 3)
            pe.wait_ge(w_loaded, 16 * 7)
            for dst, src in ((AG[0], w_raw), (AG[1], wih_raw), (R, whh_raw)):
                for i in range(3):
                    ins = nc.tensor.transpose(dst[:, P * i:P * i + P], src[:, i, :], ident[:, :])
                ins.then_inc(w_turned, 1)
            nc.tensor.transpose(Z[:, 0:6], brow, ident[0:6, 0:6]).then_inc(w_turned, 1)
            pe.wait_ge(id_made, 12)
            nc.tensor.matmul(TR[0][:, 0:E], ones_row[:, :], bg_row[:, :], start=True, stop=True).then_inc(bg_full, 1)
            pe.wait_ge(w_taken, 2)
            for l, dst in enumerate((HN, IN, AG[0])):
                ins = nc.tensor.matmul(dst[:, 0:384], wT[:, l, :], wihT, start=True, stop=True)
            ins.then_inc(w_fused, 1)

            def input_turn(nb, c, tr, k):
                pe.wait_ge(ln_xn, nb + 1)
                need(pe, tr_free, tr - 1)
                for t in range(CT):
                    ins = nc.tensor.transpose(TR[k % 2][:, P * t:P * t + P], xn[:, CT * c + t, :], ident[:, :])
                ins.then_inc(tr_full, 1)

            def aggregate(it, half, l, c, part):
                n = chunk_no(it, half, l, 0)
                g = half
                for t in range(CT * part, CT * part + CT):
                    for h in (hidden(l, hN_hi), hidden(l, hN_lo)):
                        ins = nc.tensor.matmul(AG[c][:, :], h[:, t, :], A[g][:, t, CH * c:CH * c + CH],
                                               start=(t == 0 and h is hidden(l, hN_hi)),
                                               stop=(t == T - 1 and h is hidden(l, hN_lo)))
                if part == 1:
                    ins.then_inc(ag_full, 1)

            def products(dst, w_hi, w_lo, r_hi, r_lo, start, stop):
                for i, (w, r) in enumerate(((w_hi, r_hi), (w_hi, r_lo), (w_lo, r_hi))):
                    ins = nc.tensor.matmul(dst[:, :], w, r, start=(start and i == 0), stop=(stop and i == 2))
                return ins

            def from_h(it, half, l, c):
                n = chunk_no(it, half, l, c)
                b = 2 * it + half
                if l == 0:
                    pe.wait_ge(prep_t, 4 * b + 2 * c + 2)
                else:
                    pe.wait_ge(hlo_done, 8 * it + 4 * half + 2 * (l - 1) + c + 1)
                r_hi, r_lo = hidden(l, hT_hi)[:, c, :], hidden(l, hT_lo)[:, c, :]
                need(pe, r_done, n)
                products(R, wh_hi[:, 0, :], wh_lo[:, 0, :], r_hi, r_lo, True, False)
                need(pe, z_done, n)
                products(Z, wh_hi[:, 1, :], wh_lo[:, 1, :], r_hi, r_lo, True, False)
                need(pe, t_done, n)
                products(HN, wh_hi[:, 2, :], wh_lo[:, 2, :], r_hi, r_lo, True, True).then_inc(hn_full, 1)

            def from_ag(it, half, l, c):
                n = chunk_no(it, half, l, c)
                pe.wait_ge(ag_los, n + 1)
                r_hi, r_lo = ag_hi[c][:, :], ag_lo[c][:, :]
                products(R, wi_hi[:, l, 0, :], wi_lo[:, l, 0, :], r_hi, r_lo, False, True).then_inc(r_full, 1)
                products(Z, wi_hi[:, l, 1, :], wi_lo[:, l, 1, :], r_hi, r_lo, False, True).then_inc(z_full, 1)
                need(pe, t2_done, n)
                products(IN, wi_hi[:, l, 2, :], wi_lo[:, l, 2, :], r_hi, r_lo, True, True).then_inc(in_full, 1)

            pe.wait_ge(w_taken, 5)
            for c in range(2):
                input_turn(0, c, c, c)
            pe.wait_ge(w_split, 4)

            def pair(it):
                for half in range(2):
                    b = 2 * it + half
                    for l in range(LAYERS):
                        n = chunk_no(it, half, l, 0)
                        if l > 0:
                            route.output_turn(pe, n - 2, 0, TR[0], tr_no(it, half, 2 * l))
                        if l == 0:
                            pe.wait_ge(tr_free, 2 if is_first(it, half) else tr_no(*prev(it, half), 9) + 1)
                        from_h(it, half, l, 0)
                        if l == 0:
                            pe.wait_ge(prep_lo, b + 1)
                            pe.wait_ge(a_made, 8 * b + CT)
                        else:
                            pe.wait_ge(tr_free, tr_no(it, half, 2 * l) + 1)
                        need(pe, ag_los, n - 1)
                        aggregate(it, half, l, 0, 0)
                        if l > 0:
                            route.output_turn(pe, n - 1, 1, TR[1], tr_no(it, half, 2 * l + 1))
                        elif routed(it, half):
                            route.count(pe, b - 2, TR[1], tr_no(*prev(it, half), 11))
                        need(pe, ag_los, n)
                        aggregate(it, half, l, 1, 0)
                        if l == 0 and not is_first(it, half):
                            for c in range(2):
                                route.output_turn(pe, n - 2 + c, c, TR[c], tr_no(it, half, c))
                        if l == 0:
                            pe.wait_ge(a_made, 8 * b + T)
                        else:
                            pe.wait_ge(tr_free, tr_no(it, half, 2 * l + 1) + 1)
                        aggregate(it, half, l, 0, 1)
                        if l == 2 and not is_first(it, half):
                            for c in range(2):
                                route.result_turn(pe, b - 1, 1 - half, c, TR[c], tr_no(it, half, 6 + c))
                        aggregate(it, half, l, 1, 1)
                        if l == 2 and not is_last(it, half):
                            input_turn(b + 1, 0, tr_no(it, half, 8), 0)
                        from_ag(it, half, l, 0)
                        if l == 2 and not is_last(it, half):
                            input_turn(b + 1, 1, tr_no(it, half, 9), 1)
                        from_h(it, half, l, 1)
                        if l == 2 and not is_first(it, half):
                            route.scores(pe, b - 1, TR[0], tr_no(it, half, 10), is_last(it, half))
                        from_ag(it, half, l, 1)

            loop(pe, pair)


def experts(nc, W1, b1, W2, b2, out, bank, x2, ident, sorted_x, sorted_y, route, sem):
    M = FIRST_TILE[-1]
    KT = max(ROUND_GRAPHS) * N // CH
    WW = 2 * HC * P
    LAST = route.LAST
    with ExitStack() as ctx:
        def sb(name, shape, dt=F32):
            return ctx.enter_context(nc.sbuf_tensor(name, shape, dt))

        U = bank[0:4]
        XT = bank[4]
        Y = bank[5:7]
        TR = bank[7]
        w1_raw = sb("w1_raw", [P, E, HC * P])
        w2_raw = sb("w2_raw", [P, E, HC * P])
        b_raw = sb("b_raw", [2 * E, P])
        b2_raw = sb("b2_raw", [2, E, P])
        w1_all = sb("w1_all", [P, E, WW], R32)
        w2_all = sb("w2_all", [P, E, HC, 2, P], R32)
        b1_all = sb("b1_all", [P, E, HC])
        b2_hi = sb("b2_hi", [2, E, P], R32)
        b2_all = sb("b2_all", [2, E, P], R32)
        is_low = sb("is_low", [2, 1])
        ones_f = sb("ones_f", [2, P])
        ones_r = sb("ones_r", [2, P], R32)
        w1 = [sb(f"w1_{i}", [P, WW], R32) for i in range(2)]
        bias1 = [sb(f"bias1_{i}", [P, HC]) for i in range(2)]
        tile_no_i = sb("tile_no_i", [P, max(TILES)], I32)
        full_i = sb("full_i", [P, KT], I32)
        region_i = sb("region_i", [P, E], I32)
        tile_no = sb("tile_no", [P, max(TILES)])
        full = sb("full", [P, KT])
        region = sb("e_region", [P, E])
        over = sb("over", [P, E, KT])
        tiles_of = sb("tiles_of", [P, E])
        begins = sb("begins", [P, E + 1])
        unused = sb("unused", [P, ROUNDS, E])
        passed = sb("passed", [P, max(TILES), E])
        skipped = sb("skipped", [P, max(TILES), E])
        expert_of = sb("expert_of", [P, max(TILES)])
        row_of = sb("row_of", [P, max(TILES)])
        tab_e = sb("tab_e", [P, M], I32)
        tab_x = sb("tab_x", [P, M], I32)
        row_in = sb("row_in", [P, B * T * TOP])
        row_out = sb("row_out", [P, B * T * TOP])
        row_less = sb("row_less", [P, B * T * TOP])
        y_rows = sb("y_rows", [P, B, T, TOP], I32)
        tab_pad = sb("tab_pad", [P, ROUNDS * E], I32)
        x_slot = [sb(f"x_slot{i}", [1, 1], I32) for i in range(2)]
        zeros = sb("zeros", [P, CT, P])
        xg = [sb(f"xg{i}", [P, CT, P]) for i in range(2)]
        xT_hi = [sb(f"xT_hi{i}", [P, CH], R32) for i in range(2)]
        xT_lo = [sb(f"xT_lo{i}", [P, CH], R32) for i in range(2)]
        g = [[sb(f"g{i}{c}", [P, CH]) for c in range(HC)] for i in range(2)]
        g_hi = [[sb(f"g_hi{i}{c}", [P, CH], R32) for c in range(HC)] for i in range(2)]
        g_lo = [[sb(f"g_lo{i}{c}", [P, CH], R32) for c in range(HC)] for i in range(2)]
        yo = [sb(f"yo{i}", [P, CT, P]) for i in range(2)]
        got = [sb(f"got{i}", [P, T, TOP, P]) for i in range(2)]
        fo = [sb(f"fo{i}", [P, T, P]) for i in range(2)]

        w1_in = sem("w1_in")
        w2_in = sem("w2_in")
        b_in = sem("b_in")
        made = sem("made")
        tab = sem("tab")
        tab_done = sem("tab_done")
        b_turned = sem("b_turned")
        b_taken = sem("b_taken")
        w_ready = sem("w_ready")
        padded = sem("padded")
        x_slotted = sem("x_slotted")
        y_rows_made = sem("y_rows_made")
        x_in = [sem(f"xg_in{i}") for i in range(2)]
        xt_full = sem("xt_full")
        x_hi = sem("x_hi")
        x_lo = sem("x_lo")
        w1_set = sem("w1_set")
        u_full = sem("u_full")
        g_made = sem("g_made")
        g_his = [sem(f"g_his{c}") for c in range(HC)]
        g_los = sem("g_los")
        down = sem("down")
        yo_made = sem("yo_made")
        y_stored = [sem(f"y_stored{i}") for i in range(2)]
        got_in = [sem(f"got_in{i}") for i in range(2)]
        summed = sem("summed")
        fo_made = sem("fo_made")
        out_stored = [sem(f"out_stored{i}") for i in range(2)]
        e_passed = sem("e_passed")

        block = ctx.enter_context(nc.Block())

        ROUTED = 6
        SUM_STEPS = [FIRST_TILE[1] + 5 + 4 * q for q in range(4)]
        SUM_AT = (SUM_STEPS[0] - 1) // 2 * 2
        LOOP_END = (M - 4) // 2 * 2

        def round_at(m):
            return 0 if m < FIRST_TILE[1] else 1

        def there(m):
            return not isinstance(m, int) or 0 <= m < M

        def evens(m, p):
            return 2 * (m // 2) if not isinstance(m, int) else m - p

        def loop(eng, step, end):
            for n in range(-3, ROUTED):
                step(n, n % 2)
            with eng.Fori(ROUTED // 2, end // 2) as i:
                for k in range(2):
                    step(2 * i + k, k)
            for n in range(end, M + 1):
                step(n, n % 2)

        @block.sync
        def _(sp):
            sp.dma_start(w1_raw[:, :, :], W1.rearrange("e d h -> d e h")).then_inc(w1_in, 16)
            sp.dma_start(b_raw[:, :], b1.rearrange("e (c j) -> (e c) j", j=P)).then_inc(b_in, 16)
            for i in range(2):
                sp.dma_start(b2_raw[i:i + 1, :, :], b2.rearrange("(o e) d -> o e d", o=1)).then_inc(b_in, 16)
            sp.wait_ge(made, 1)
            for r in range(ROUNDS):
                sp.dma_start(sorted_x[r][SPARE:SPARE + CH, :].rearrange("(p t) d -> p t d", p=P), zeros[:, :, :]).then_inc(padded, 16)

            def pad(r):
                sp.wait_ge(tab_done, r + 1)
                sp.wait_ge(route.scattered, 16 * TOP * T * FIRST_GRAPH[r + 1])
                for n in range(E * r, E * r + E):
                    row = nc.values_load(tab_pad[0:1, n:n + 1], engines=[mybir.EngineType.SP], min_val=0, max_val=SPARE)
                    sp.dma_start(sorted_x[r][bass.ds(row, CH), :].rearrange("(p t) d -> p t d", p=P), zeros[:, :, :]).then_inc(padded, 16)
                sp.wait_ge(padded, 16 * (ROUNDS + E * (r + 1)))

            def step(n, k, r_in, r_out):
                m = n + 3
                if there(m):
                    p = 1 - k
                    sp.wait_ge(x_slotted, m + 1)
                    sp.sem_inc(e_passed, 1)
                    need(sp, xt_full, m - 1)
                    sp.sem_inc(e_passed, 1)
                    row = nc.values_load(x_slot[p][:, :], engines=[mybir.EngineType.SP], min_val=0, max_val=SPARE)
                    sp.dma_start(xg[p][:, :, :], sorted_x[r_in][bass.ds(row, CH), :].rearrange("(p t) d -> p t d", p=P)).then_inc(x_in[p], 16)
                m = n - 1
                if there(m):
                    p = 1 - k
                    sp.wait_ge(yo_made, m + 1)
                    at = m - FIRST_TILE[r_out]
                    dst = sorted_y[r_out][CH * at:CH * at + CH, :] if isinstance(m, int) else sorted_y[r_out][bass.ds(CH * at, CH), :]
                    sp.dma_start(dst.rearrange("(p t) d -> p t d", p=P), yo[p][:, :, :]).then_inc(y_stored[p], 16)

            pad(0)
            N1 = FIRST_TILE[1]
            for n in range(-3, ROUTED):
                step(n, n % 2, 0, 0)
            with sp.Fori(ROUTED // 2, (N1 - 4) // 2) as i:
                for k in range(2):
                    step(2 * i + k, k, 0, 0)
            for n in range((N1 - 4) // 2 * 2, N1 + 2):
                if n == N1 - 3:
                    pad(1)
                step(n, n % 2, round_at(n + 3), round_at(n - 1))
            with sp.Fori(N1 // 2 + 1, LOOP_END // 2) as i:
                for k in range(2):
                    step(2 * i + k, k, 1, 1)
            for n in range(LOOP_END, M + 1):
                step(n, n % 2, 1, 1)

        @block.gpsimd
        def _(pool):
            nc.gpsimd.memset(zeros[:, :, :], 0.0).then_inc(made, 1)
            nc.gpsimd.iota(tile_no_i[:, :], pattern=[[1, max(TILES)]], base=0, channel_multiplier=0).then_inc(made, 1)
            nc.gpsimd.iota(full_i[:, :], pattern=[[CH, KT]], base=0, channel_multiplier=0).then_inc(made, 1)
            nc.gpsimd.iota(region_i[:, :], pattern=[[REG, E]], base=0, channel_multiplier=0).then_inc(made, 1)
            nc.gpsimd.memset(ones_f[:, :], 1.0).then_inc(made, 1)
            nc.gpsimd.memset(is_low[:, :], -1.0).then_inc(made, 1)
            pool.wait_ge(made, 6)
            nc.gpsimd.memset(is_low[0:1, :], 0.0).then_inc(made, 1)
            route.scatter(pool, B - 2, 0, 0, 4)
            route.scale(pool, B - 1)
            route.scatter(pool, B - 2, 0, 4, T)
            route.scatter(pool, B - 1, 1, 0, T)
            for q in range(B):
                p = q % 2
                r = round_of(q)
                if q == FIRST_GRAPH[r]:
                    pool.wait_ge(y_rows_made, r + 1)
                    for k in range(2):
                        pool.wait_ge(y_stored[k], 8 * FIRST_TILE[r + 1])
                    pool.sem_inc(route.pool_passed, 1)
                need(pool, summed, 2 * (q - 2) + 1)
                pool.sem_inc(route.pool_passed, 1)
                for t in range(T):
                    for j in range(TOP):
                        nc.gpsimd.indirect_dma_start(
                            out=got[p][:, t, j, :], out_offset=None, in_=sorted_y[r],
                            in_offset=bass.IndirectOffsetOnAxis(ap=y_rows[:, q, t, j:j + 1].bitcast(U32), axis=0)).then_inc(got_in[p], 16)

        @block.scalar
        def _(act):
            act.dma_start(w2_raw[:, :, :].rearrange("p e (c d) -> p e c d", c=HC), W2.rearrange("e (c h) d -> h e c d", h=P)).then_inc(w2_in, 16)

            def step(n, k):
                m = n + 2
                if there(m):
                    act.wait_ge(xt_full, m + 1)
                    need(act, u_full, 2 * m - 2)
                    nc.scalar.activation(xT_hi[k][:, :], XT[:, :], ACT.Copy).then_inc(x_hi, 1)
                m = n + 1
                if there(m):
                    p = 1 - k
                    for c in range(HC):
                        act.wait_ge(u_full, 2 * m + c + 1)
                        need(act, g_los, 2 * m + c - 3)
                        nc.scalar.activation(g[p][c][:, :], U[2 * p + c][:, :], ACT.Gelu, bias=bias1[p][:, c:c + 1]).then_inc(g_made, 1)
                    act.wait_ge(g_made, 2 * m + 1)
                    need(act, down, m - 1)
                    nc.scalar.activation(g_hi[p][0][:, :], g[p][0][:, :], ACT.Copy).then_inc(g_his[0], 1)
                if isinstance(n, int):
                    if n == -2:
                        route.apply(act, B - 1, 1)
                    if n in (-1, 0):
                        route.turned(act, B - 1, n + 1, TR, LAST + n + 3)
                    if n - 1 in SUM_STEPS:
                        store(SUM_STEPS.index(n - 1))

            def store(q):
                act.wait_ge(fo_made, q + 1)
                act.dma_start(out.rearrange("b (t p) d -> b p t d", p=P)[q, :, :, :], fo[q % 2][:, :, :]).then_inc(out_stored[q % 2], 16)

            loop(act, step, SUM_AT)
            for q in range(len(SUM_STEPS), B):
                store(q)
            for k in range(2):
                act.wait_ge(out_stored[k], 16 * B // 2)

        @block.vector
        def _(dve):
            m = [0]

            def then(ins):
                m[0] += 1
                ins.then_inc(tab, 1)
                dve.wait_ge(tab, m[0])

            AX = mybir.AxisListType.X

            def table(r):
                NT = TILES[r]
                count = route.counts[:, FIRST_GRAPH[r + 1] - 1, :]
                then(nc.vector.tensor_tensor(over[:, :, :], count.rearrange("p (e o) -> p e o", o=1).to_broadcast([P, E, KT]),
                                             full[:, :].rearrange("p (o k) -> p o k", o=1).to_broadcast([P, E, KT]), ALU.is_gt))
                then(nc.vector.tensor_reduce(tiles_of[:, :], over[:, :, :], AX, ALU.add))
                then(nc.vector.memset(begins[:, 0:1], 0.0))
                for e in range(E):
                    then(nc.vector.tensor_tensor(begins[:, e + 1:e + 2], begins[:, e:e + 1], tiles_of[:, e:e + 1], ALU.add))
                then(nc.vector.tensor_scalar(unused[:, r, :], tiles_of[:, :], -float(CH), float(REG), ALU.mult, ALU.add))
                nr = tile_no[:, 0:NT].rearrange("p (n o) -> p n o", o=1).to_broadcast([P, NT, E])
                er = begins[:, 1:E + 1].rearrange("p (o e) -> p o e", o=1).to_broadcast([P, NT, E])
                ur = unused[:, r, :].rearrange("p (o e) -> p o e", o=1).to_broadcast([P, NT, E])
                at = slice(FIRST_TILE[r], FIRST_TILE[r + 1])
                then(nc.vector.tensor_tensor(passed[:, 0:NT, :], nr, er, ALU.is_ge))
                then(nc.vector.tensor_tensor(skipped[:, 0:NT, :], passed[:, 0:NT, :], ur, ALU.mult))
                then(nc.vector.tensor_reduce(expert_of[:, 0:NT], passed[:, 0:NT, :], AX, ALU.add))
                then(nc.vector.tensor_reduce(row_of[:, 0:NT], skipped[:, 0:NT, :], AX, ALU.add))
                then(nc.vector.scalar_tensor_tensor(out=row_of[:, 0:NT], in0=tile_no[:, 0:NT], scalar=float(CH), in1=row_of[:, 0:NT],
                                                    op0=ALU.mult, op1=ALU.add))
                then(nc.vector.tensor_scalar(tab_x[:, at], row_of[:, 0:NT], float(SPARE), None, ALU.min))
                then(nc.vector.tensor_scalar(tab_e[:, at], expert_of[:, 0:NT], float(E - 1), None, ALU.min))
                then(nc.vector.tensor_tensor(tab_pad[:, E * r:E * r + E], count, region[:, :], ALU.add))
                dve.sem_inc(tab_done, 1)

            dve.wait_ge(made, 7)
            nc.vector.tensor_copy(tile_no[:, :], tile_no_i[:, :])
            nc.vector.tensor_copy(full[:, :], full_i[:, :])
            nc.vector.tensor_copy(ones_r[:, :], ones_f[:, :])
            then(nc.vector.tensor_copy(region[:, :], region_i[:, :]))
            route.places(dve, B - 2, TR, LAST - 1)
            for c in range(2):
                route.residual(dve, B - 1, c, TR, LAST + c)
            table(0)
            route.norm(dve, B - 1, LAST + 1)
            dve.wait_ge(b_turned, 1)
            dve.wait_ge(b_in, 48)
            nc.vector.tensor_copy(b1_all[:, :, :].rearrange("p e c -> p (e c)"), XT[:, 0:2 * E]).then_inc(b_taken, 1)
            nc.vector.tensor_copy(b2_hi[:, :, :], b2_raw[:, :, :])
            dve.wait_ge(w1_in, 16)
            then(nc.vector.tensor_copy(w1_all[:, :, 0:HC * P], w1_raw[:, :, :]))
            nc.vector.scalar_tensor_tensor(out=b2_all[:, :, :], in0=f32(b2_hi[:, :, :]), scalar=is_low[:, 0:1], in1=b2_raw[:, :, :],
                                           op0=ALU.mult, op1=ALU.add)
            then(nc.vector.tensor_tensor(w1_all[:, :, HC * P:WW], w1_raw[:, :, :], f32(w1_all[:, :, 0:HC * P]), ALU.subtract))

            def second_weights():
                dve.wait_ge(w2_in, 16)
                raw = w2_raw[:, :, :].rearrange("p e (c d) -> p e c d", c=HC)
                then(nc.vector.tensor_copy(w2_all[:, :, :, 0, :], raw))
                nc.vector.tensor_tensor(w2_all[:, :, :, 1, :], raw, f32(w2_all[:, :, :, 0, :]), ALU.subtract).then_inc(w_ready, 1)

            def of(table, m):
                return table[0:1, m:m + 1] if isinstance(m, int) else table[0:1, bass.ds(m, 1)]

            def step(n, k):
                m = n - 1
                if there(m):
                    p = 1 - k
                    dve.wait_ge(down, m + 1)
                    need(dve, y_stored[p], 8 * evens(m, p))
                    nc.vector.tensor_copy(yo[p][:, :, :], Y[p][:, :].rearrange("p (t d) -> p t d", t=CT)).then_inc(yo_made, 1)
                m = n + 2
                if there(m):
                    dve.wait_ge(x_hi, m + 1)
                    nc.vector.tensor_tensor(xT_lo[k][:, :], XT[:, :], f32(xT_hi[k][:, :]), ALU.subtract).then_inc(x_lo, 1)
                    e = nc.values_load(of(tab_e, m), engines=[mybir.EngineType.DVE], min_val=0, max_val=E - 1)
                    need(dve, g_made, 2 * m - 2)
                    dve.sem_inc(e_passed, 1)
                    nc.vector.tensor_copy(bias1[k][:, :], b1_all[:, bass.ds(e, 1), :].rearrange("p o c -> p (o c)"))
                    nc.vector.tensor_copy(w1[k][:, :], f32(w1_all[:, bass.ds(e, 1), :].rearrange("p o c -> p (o c)"))).then_inc(w1_set, 1)
                m = n + 3
                if there(m):
                    p = 1 - k
                    need(dve, x_in[p], 8 * evens(m, p))
                    dve.sem_inc(e_passed, 1)
                    nc.vector.tensor_copy(x_slot[p][:, :], of(tab_x, m)).then_inc(x_slotted, 1)
                m = n + 1
                if there(m):
                    p = 1 - k
                    dve.wait_ge(g_his[0], m + 1)
                    need(dve, down, m - 1)
                    nc.vector.tensor_tensor(g_lo[p][0][:, :], g[p][0][:, :], f32(g_hi[p][0][:, :]), ALU.subtract).then_inc(g_los, 1)
                    dve.wait_ge(g_made, 2 * m + 2)
                    nc.vector.tensor_copy(g_hi[p][1][:, :], g[p][1][:, :]).then_inc(g_his[1], 1)
                    dve.wait_ge(g_his[1], m + 1)
                    nc.vector.tensor_tensor(g_lo[p][1][:, :], g[p][1][:, :], f32(g_hi[p][1][:, :]), ALU.subtract).then_inc(g_los, 1)
                if isinstance(n, int):
                    if n == -3:
                        second_weights()
                    if n == 1:
                        route.gates(dve, B - 1, TR, LAST + 4)
                    if n == 2:
                        route.places(dve, B - 1, TR, LAST + 5)
                    if n == 3:
                        table(1)
                    if n in (4, 5):
                        result_rows(n - 4)
                    if n in SUM_STEPS:
                        q = SUM_STEPS.index(n)
                        total(q, q % 2)

            def result_rows(r):
                w = T * TOP
                at = slice(w * FIRST_GRAPH[r], w * FIRST_GRAPH[r + 1])
                nc.vector.tensor_copy(row_in[:, at], route.slots[:, at])
                then(nc.vector.tensor_copy(row_out[:, at], route.slots[:, at]))
                for e in range(1, E):
                    then(nc.vector.tensor_scalar(row_less[:, at], row_in[:, at], float(e * REG), unused[:, r, e - 1:e], ALU.is_ge, ALU.mult))
                    then(nc.vector.tensor_tensor(row_out[:, at], row_out[:, at], row_less[:, at], ALU.subtract))
                nc.vector.tensor_copy(y_rows[:, FIRST_GRAPH[r]:FIRST_GRAPH[r + 1], :, :].rearrange("p b t k -> p (b t k)"),
                                      row_out[:, at]).then_inc(y_rows_made, 1)

            def total(q, p):
                whole_q = T * q
                mine = x2[:, whole_q:whole_q + T, :] if isinstance(q, int) else x2[:, bass.ds(whole_q, T), :]
                dve.wait_ge(got_in[p], 256 * (q // 2 + 1))
                need(dve, out_stored[p], 16 * (q // 2))
                nc.vector.tensor_tensor(fo[p][:, :, :], got[p][:, :, 0, :], got[p][:, :, 1, :], ALU.add).then_inc(summed, 1)
                dve.wait_ge(summed, 2 * q + 1)
                nc.vector.tensor_tensor(fo[p][:, :, :], fo[p][:, :, :], mine, ALU.add).then_inc(fo_made, 1)
                dve.sem_inc(summed, 1)

            loop(dve, step, SUM_AT)
            for q in range(len(SUM_STEPS), B):
                total(q, q % 2)

        @block.tensor
        def _(pe):
            route.count(pe, B - 2, TR, LAST - 1, True)
            for c in range(2):
                route.output_turn(pe, 6 * B - 2 + c, c, TR, LAST + c, True)
            pe.wait_ge(b_in, 48)
            nc.tensor.transpose(XT[:, 0:2 * E], b_raw[:, :], ident[0:2 * E, 0:2 * E]).then_inc(b_turned, 1)
            pe.wait_ge(tab_done, 1)

            def step(n, k):
                m = n + 2
                if there(m):
                    pe.wait_ge(x_in[k], 16 + 8 * evens(m, k))
                    need(pe, x_lo, m)
                    if isinstance(m, int) and m == 0:
                        pe.wait_ge(b_taken, 1)
                    for t in range(CT):
                        ins = nc.tensor.transpose(XT[:, P * t:P * t + P], xg[k][:, t, :], ident[:, :])
                    ins.then_inc(xt_full, 1)
                m = n + 1
                if there(m):
                    p = 1 - k
                    pe.wait_ge(w1_set, m + 1)
                    pe.wait_ge(x_lo, m + 1)
                    for c in range(HC):
                        need(pe, g_made, 2 * m + c - 3)
                        hi, lo = w1[p][:, P * c:P * c + P], w1[p][:, HC * P + P * c:HC * P + P * c + P]
                        for i, (w, r) in enumerate(((hi, xT_hi), (hi, xT_lo), (lo, xT_hi))):
                            ins = nc.tensor.matmul(U[2 * p + c][:, :], w, r[p][:, :], start=(i == 0), stop=(i == 2))
                        ins.then_inc(u_full, 1)
                m = n
                if there(m):
                    at = tab_e[0:1, m:m + 1] if isinstance(m, int) else tab_e[0:1, bass.ds(m, 1)]
                    e = nc.values_load(at, engines=[mybir.EngineType.PE], min_val=0, max_val=E - 1)
                    if isinstance(m, int) and m == 0:
                        pe.wait_ge(w_ready, 1)
                    pe.wait_ge(g_los, 2 * m + 2)
                    need(pe, yo_made, m - 1)
                    nc.tensor.matmul(Y[k][:, :].rearrange("p (t d) -> p t d", t=CT), ones_r[:, :],
                                     b2_all[:, bass.ds(e, 1), :].to_broadcast([2, CT, P]), start=True, stop=False)
                    for t in range(CT):
                        for c in range(HC):
                            for gh, half in ((g_hi, 0), (g_hi, 1), (g_lo, 0)):
                                ins = nc.tensor.matmul(Y[k][:, P * t:P * t + P], gh[k][c][:, P * t:P * t + P],
                                                       w2_all[:, bass.ds(e, 1), c, half, :].rearrange("p o d -> p (o d)"),
                                                       start=False, stop=(t == CT - 1 and c == HC - 1 and gh is g_lo))
                    ins.then_inc(down, 1)
                if isinstance(n, int):
                    if n in (-1, 0):
                        route.result_turn(pe, B - 1, 1, n + 1, TR, LAST + n + 3, True)
                    if n == 1:
                        route.scores(pe, B - 1, TR, LAST + 4, True)
                    if n == 2:
                        route.count(pe, B - 1, TR, LAST + 5, True)

            loop(pe, step, LOOP_END)


_INS = ['x', 'adj', 'L0_gnn_weight', 'L0_gnn_w_ih', 'L0_gnn_w_hh', 'L0_gnn_b_ih', 'L0_gnn_b_hh', 'L0_ffn_Wg',
        'L0_ffn_bg', 'L0_ffn_W1', 'L0_ffn_b1', 'L0_ffn_W2', 'L0_ffn_b2']


def kernel(**inputs):
    import numpy as _np
    import concourse.bacc as _bacc
    from concourse import mybir as _mybir
    from concourse.bass_utils import run_bass_kernel_spmd as _run

    nc = _bacc.Bacc("TRN2", target_bir_lowering=False, num_devices=1)
    arrays, args = {}, []
    for name in _INS:
        a = _np.ascontiguousarray(inputs[name])
        arrays[f"in_{name}_dram"] = a
        args.append(nc.dram_tensor(f"in_{name}_dram", a.shape, _mybir.dt.from_np(a.dtype), kind="ExternalInput").ap())
    args.append(nc.dram_tensor("out_0_dram", (8, 1024, 128), _mybir.dt.float32, kind="ExternalOutput").ap())
    gnn_ffn(nc, *args)
    r = _run(nc, [arrays], core_ids=[0])
    return r.results[0]["out_0_dram"]
```

```python
import concourse.bass as bass
from concourse import mybir
from contextlib import ExitStack

F32 = mybir.dt.float32
R32 = mybir.dt.float32r
I32 = mybir.dt.int32
U32 = mybir.dt.uint32
BF16 = mybir.dt.bfloat16
ALU = mybir.AluOpType
ACT = mybir.ActivationFunctionType

P = 128
B = 8
N = 1024
T = N // P
LAYERS = 3
CH = 512
CT = CH // P
EPS = 1e-5
STG = 4


def f32(ap):
    return ap.bitcast(F32)


def need(eng, sem, value):
    if isinstance(value, int) and value <= 0:
        return
    eng.wait_ge(sem, value)


E = 8
HC = 2
TOP = 2
ROUND_GRAPHS = (5, 3)
ROUNDS = len(ROUND_GRAPHS)
FIRST_GRAPH = [sum(ROUND_GRAPHS[:r]) for r in range(ROUNDS + 1)]
REG = max(ROUND_GRAPHS) * N + CH
TILES = [n * N * TOP // CH + E - 1 for n in ROUND_GRAPHS]
FIRST_TILE = [sum(TILES[:r]) for r in range(ROUNDS + 1)]
SPARE = E * REG
RS = SPARE + max(TILES) * CH


def round_of(b):
    return 0 if not isinstance(b, int) else sum(b >= g for g in FIRST_GRAPH[1:ROUNDS])




def gnn_ffn(nc, x, adj, weight, w_ih, w_hh, b_ih, b_hh, Wg, bg, W1, b1, W2, b2, out):
    with ExitStack() as whole:
        def sb(name, shape, dt=F32):
            return whole.enter_context(nc.sbuf_tensor(name, shape, dt))

        def sem(name):
            return whole.enter_context(nc.semaphore(name))

        bank = [whole.enter_context(nc.psum_tensor(f"bank{i}", [P, CH], F32)) for i in range(8)]
        x2 = sb("x2", [P, B * T, P])
        ident = sb("ident", [P, P])
        sorted_x = [nc.dram_tensor(f"sorted_x{r}", (RS, P), F32, kind="Internal").ap() for r in range(ROUNDS)]
        sorted_y = [nc.dram_tensor(f"sorted_y{r}", (TILES[r] * CH, P), F32, kind="Internal").ap() for r in range(ROUNDS)]
        stage = sb("stage", [P, STG, N], I32)
        first_a = sb("A0", [P, T, N], R32)
        route = Routing(nc, sb, sem, x2, ident, sorted_x)
        weights = Weights(nc, sem, W1, W2, stage, first_a)
        plan = Plan(nc, sb, sem, route, sorted_x)
        graphs(nc, x, adj, weight, w_ih, w_hh, b_ih, b_hh, Wg, bg, bank, x2, ident, stage, first_a, weights, route, plan, sem)
        experts(nc, weights, b1, b2, out, bank, x2, ident, sorted_x, sorted_y, route, plan, sem)


class Routing:

    LAST = 12 * B - 6

    def __init__(self, nc, sb, sem, x2, ident, sorted_x):
        self.nc, self.x2, self.ident, self.sorted_x = nc, x2, ident, sorted_x
        self.h_last = sb("hT1", [P, 2, CH])
        self.xr = [sb(f"xr{i}", [P, T, P]) for i in range(2)]
        self.xrT = sb("xrT", [P, 2, CH])
        self.st = sb("r_st", [P, T, 6])
        self.mean_var = sb("r_mean_var", [P, T, 2])
        self.veps = sb("r_veps", [P, T])
        self.rstd = sb("r_rstd", [P, T])
        self.shift = sb("r_shift", [P, T])
        self.mhalf = sb("mhalf", [P, T])
        self.wg = sb("wg", [P, E])
        self.bgb = sb("bgb", [P, E])
        self.ones = sb("ones", [P, P], BF16)
        self.earlier = sb("earlier", [P, P], BF16)
        self.sc = sb("sc", [P, T, E])
        self.beats = sb("beats", [P, T, E, E], BF16)
        self.ties = sb("ties", [P, T, E, E], BF16)
        self.before = sb("before", [P, E, E], BF16)
        self.rank = sb("rank", [P, T, E])
        self.sel = sb("sel", [P, T, E])
        self.sel_bf = sb("sel_bf", [P, T + 1, E], BF16)
        self.offset = sb("offset", [P, E])
        self.pos = sb("pos", [P, T, E])
        self.region = sb("region", [P, T, E])
        self.keep_count = sb("keep_count", [P, B])
        self.high_row = sb("high_row", [P, T])
        self.both_rows = sb("both_rows", [P, T])
        self.rows_now = sb("rows_now", [P, T, TOP], I32)
        self.slots = sb("slots", [P, B * T * TOP], I32)
        self.counts = sb("counts", [P, B, E])
        self.pool_passed = sem("pool_passed")
        self.dve_passed = sem("dve_passed")
        self.h_done = sem("h_done")
        self.tr_full = sem("tr_full")
        self.tr_free = sem("tr_free")
        self.r_stats = sem("r_stats")
        self.r_mv = sem("r_mv")
        self.r_scale_in = sem("r_scale_in")
        self.r_scale = sem("r_scale")
        self.r_xr = sem("r_xr")
        self.gate = sem("gate")
        self.placed = sem("placed")
        self.rows_made = sem("rows_made")
        self.scattered = sem("scattered")

    def tile(self, b, t, n=1):
        at = T * b + t
        v = self.x2[:, at:at + n, :] if isinstance(at, int) else self.x2[:, bass.ds(at, n), :]
        return v.rearrange("p o d -> p (o d)") if n == 1 else v

    def per_graph(self, v, b, n=1):
        return v[:, n * b:n * b + n] if isinstance(b, int) else v[:, bass.ds(n * b, n)]


    def output_turn(self, pe, n, c, bank, tr, alone=False):
        pe.wait_ge(self.h_done, n + 1)
        need(pe, self.tr_free, tr if alone else tr - 1)
        for t in range(CT):
            ins = self.nc.tensor.transpose(bank[:, P * t:P * t + P], self.h_last[:, c, P * t:P * t + P], self.ident[:, :])
        ins.then_inc(self.tr_full, 1)

    def result_turn(self, pe, b, half, c, bank, tr, alone=False):
        pe.wait_ge(self.r_xr, b + 1)
        pe.wait_ge(self.tr_free, tr if alone else tr - 1)
        for t in range(CT):
            ins = self.nc.tensor.transpose(bank[:, P * t:P * t + P], self.xr[half][:, CT * c + t, :], self.ident[:, :])
        ins.then_inc(self.tr_full, 1)

    def scores(self, pe, b, bank, tr, alone=False):
        pe.wait_ge(self.tr_free, tr if alone else tr - 1)
        for t in range(T):
            ins = self.nc.tensor.matmul(bank[:, E * t:E * t + E], self.xrT[:, t // CT, P * (t % CT):P * (t % CT) + P],
                                        self.wg[:, :], start=True, stop=True)
        ins.then_inc(self.tr_full, 1)

    def count(self, pe, b, bank, tr, alone=False):
        pe.wait_ge(self.gate, 7 * b + 6)
        pe.wait_ge(self.tr_free, tr if alone else tr - 1)
        self.nc.tensor.matmul(bank[:, 0:T * E + E], self.earlier[:, :], self.sel_bf[:, :, :].rearrange("p t e -> p (t e)"),
                              start=True, stop=False)
        for t in range(T):
            n = T - t
            ins = self.nc.tensor.matmul(bank[:, E * t + E:T * E + E], self.ones[:, :],
                                        self.sel_bf[:, t:t + 1, :].to_broadcast([P, n, E]),
                                        start=False, stop=(t == T - 1))
        ins.then_inc(self.tr_full, 1)


    def scale(self, pool, b):
        pool.wait_ge(self.r_scale_in, b + 1)
        self.nc.gpsimd.tensor_tensor(self.rstd[:, :], self.veps[:, :], self.mhalf[:, :], ALU.pow).then_inc(self.r_scale, 1)
        pool.wait_ge(self.r_scale, 2 * b + 1)
        self.nc.gpsimd.tensor_tensor(self.shift[:, :], self.shift[:, :], self.rstd[:, :], ALU.mult).then_inc(self.r_scale, 1)

    def scatter(self, pool, b, half, first, end):
        pool.wait_ge(self.rows_made, b + 1)
        pool.sem_inc(self.pool_passed, 1)
        for t in range(first, end):
            for k in range(TOP):
                self.nc.gpsimd.indirect_dma_start(
                    out=self.sorted_x[round_of(b)],
                    out_offset=bass.IndirectOffsetOnAxis(ap=self.rows_now[:, t, k:k + 1].bitcast(U32), axis=0),
                    in_=self.xr[half][:, t, :], in_offset=None).then_inc(self.scattered, 16)


    def normalise(self, b, dst, rs, sh, done):
        for t in range(T):
            ins = self.nc.scalar.activation(dst[:, t, :], self.tile(b, t), ACT.Identity, bias=sh[:, t:t + 1], scale=rs[:, t:t + 1])
        ins.then_inc(done, 1)

    def apply(self, act, b, half):
        act.wait_ge(self.r_scale, 2 * b + 2)
        need(act, self.scattered, 16 * TOP * T * (b - 1))
        self.normalise(b, self.xr[half], self.rstd, self.shift, self.r_xr)

    def turned(self, act, b, c, bank, tr):
        act.wait_ge(self.tr_full, tr + 1)
        need(act, self.gate, 7 * (b - 1) + 1)
        self.nc.scalar.activation(self.xrT[:, c, :], bank[:, :], ACT.Copy).then_inc(self.tr_free, 1)


    def moments(self, dve, b, st, m, ve, sh, s_stats, s_mv, s_veps):
        nc = self.nc
        dve.sem_inc(self.dve_passed, 1)
        for t in range(T):
            ins = nc.vector.bn_stats(st[:, t, :], self.tile(b, t))
        ins.then_inc(s_stats, 1)
        dve.wait_ge(s_stats, b + 1)
        dve.sem_inc(self.dve_passed, 1)
        for t in range(T):
            ins = nc.vector.bn_aggr(m[:, t, :], st[:, t, :])
        ins.then_inc(s_mv, 1)
        dve.wait_ge(s_mv, b + 1)
        nc.vector.tensor_scalar(sh[:, :], m[:, :, 0], -1.0, None, ALU.mult)
        nc.vector.tensor_scalar(ve[:, :], m[:, :, 1], EPS, None, ALU.add).then_inc(s_veps, 1)

    def residual(self, dve, b, c, bank, tr):
        dve.wait_ge(self.tr_full, tr + 1)
        self.nc.vector.tensor_tensor(self.tile(b, CT * c, CT), bank[:, :].rearrange("p (t d) -> p t d", t=CT),
                                     self.tile(b, CT * c, CT), ALU.add).then_inc(self.tr_free, 1)

    def norm(self, dve, b, tr):
        dve.wait_ge(self.tr_free, tr + 1)
        need(dve, self.r_xr, b)
        self.moments(dve, b, self.st, self.mean_var, self.veps, self.shift, self.r_stats, self.r_mv, self.r_scale_in)

    def gates(self, dve, b, bank, tr):
        self.compare(dve, b, bank, tr)
        self.break_ties(dve, b)
        self.select(dve, b)

    def compare(self, dve, b, bank, tr):
        nc = self.nc
        beats, ties = self.beats, self.ties
        dve.wait_ge(self.tr_full, tr + 1)
        nc.vector.tensor_tensor(self.sc[:, :, :], bank[:, 0:T * E].rearrange("p (t e) -> p t e", t=T),
                                self.bgb[:, :].rearrange("p (o e) -> p o e", o=1).to_broadcast([P, T, E]),
                                ALU.add).then_inc(self.tr_free, 1)
        dve.wait_ge(self.tr_free, tr + 1)
        mine = self.sc[:, :, :].rearrange("p t (i o) -> p t i o", o=1).to_broadcast([P, T, E, E])
        other = self.sc[:, :, :].rearrange("p t (o j) -> p t o j", o=1).to_broadcast([P, T, E, E])
        nc.vector.tensor_tensor(ties[:, :, :, :], other, mine, ALU.is_equal).then_inc(self.gate, 1)
        nc.vector.tensor_tensor(beats[:, :, :, :], other, mine, ALU.is_gt).then_inc(self.gate, 1)

    def break_ties(self, dve, b):
        nc = self.nc
        m = 7 * b
        beats, ties = self.beats, self.ties
        lower = self.before[:, :, :].rearrange("p (o i) j -> p o (i j)", o=1).to_broadcast([P, T, E * E])
        flat = ties[:, :, :, :].rearrange("p t i j -> p t (i j)")
        dve.wait_ge(self.gate, m + 1)
        nc.vector.tensor_tensor(flat, flat, lower, ALU.mult).then_inc(self.gate, 1)
        dve.wait_ge(self.gate, m + 3)
        nc.vector.tensor_tensor(beats[:, :, :, :], beats[:, :, :, :], ties[:, :, :, :], ALU.add).then_inc(self.gate, 1)

    def select(self, dve, b):
        nc = self.nc
        m = 7 * b
        rank = self.rank
        dve.wait_ge(self.gate, m + 4)
        nc.vector.tensor_reduce(rank[:, :, :], self.beats[:, :, :, :], mybir.AxisListType.X, ALU.add).then_inc(self.gate, 1)
        dve.wait_ge(self.gate, m + 5)
        nc.vector.tensor_scalar(self.sel_bf[:, 0:T, :], rank[:, :, :], TOP - 0.5, None, ALU.is_lt).then_inc(self.gate, 1)
        nc.vector.tensor_scalar(self.sel[:, :, :], rank[:, :, :], TOP - 0.5, None, ALU.is_lt).then_inc(self.gate, 1)

    def places(self, dve, b, bank, tr):
        nc = self.nc
        m = 8 * b
        pos = self.pos
        nc.vector.tensor_scalar(self.offset[:, :], self.offset[:, :], self.per_graph(self.keep_count, b), None,
                                ALU.mult).then_inc(self.placed, 1)
        dve.wait_ge(self.placed, m + 1)
        dve.wait_ge(self.tr_full, tr + 1)
        so_far = self.offset[:, :].rearrange("p (o e) -> p o e", o=1).to_broadcast([P, T, E])
        nc.vector.tensor_tensor(pos[:, :, :], bank[:, 0:T * E].rearrange("p (t e) -> p t e", t=T), so_far,
                                ALU.add).then_inc(self.placed, 1)
        nc.vector.tensor_tensor(self.per_graph(self.counts[:, :, :].rearrange("p b e -> p (b e)"), b, E),
                                bank[:, T * E:T * E + E], self.offset[:, :], ALU.add).then_inc(self.placed, 1)
        dve.wait_ge(self.placed, m + 2)
        nc.vector.tensor_tensor(pos[:, :, :], pos[:, :, :], self.region[:, :, :], ALU.add).then_inc(self.placed, 1)
        dve.wait_ge(self.placed, m + 3)
        nc.vector.tensor_tensor(self.offset[:, :], bank[:, T * E:T * E + E], self.offset[:, :], ALU.add).then_inc(self.tr_free, 1)
        dve.wait_ge(self.placed, m + 4)
        dve.wait_ge(self.gate, 7 * b + 7)
        nc.vector.tensor_tensor(pos[:, :, :], pos[:, :, :], self.sel[:, :, :], ALU.mult).then_inc(self.placed, 1)
        dve.wait_ge(self.placed, m + 5)
        nc.vector.tensor_reduce(self.high_row[:, :], pos[:, :, :], mybir.AxisListType.X, ALU.max)
        nc.vector.tensor_reduce(self.both_rows[:, :], pos[:, :, :], mybir.AxisListType.X, ALU.add).then_inc(self.placed, 1)
        dve.wait_ge(self.placed, m + 6)
        need(dve, self.scattered, 16 * TOP * T * b)
        nc.vector.scalar_tensor_tensor(out=self.rows_now[:, :, 0], in0=self.both_rows[:, :], scalar=-1.0, in1=self.high_row[:, :],
                                       op0=ALU.add, op1=ALU.subtract)
        nc.vector.tensor_scalar(self.rows_now[:, :, 1], self.high_row[:, :], -1.0, None, ALU.add).then_inc(self.placed, 1)
        dve.wait_ge(self.placed, m + 7)
        nc.vector.tensor_copy(self.per_graph(self.slots, b, T * TOP),
                              self.rows_now[:, :, :].rearrange("p t k -> p (t k)")).then_inc(self.placed, 1)
        dve.wait_ge(self.placed, m + 8)
        dve.wait_ge(self.tr_free, tr + 1)
        dve.sem_inc(self.rows_made, 1)
class Plan:

    SCRATCH = T * P
    KT = max(ROUND_GRAPHS) * N // CH

    def __init__(self, nc, sb, sem, route, sorted_x):
        most = max(TILES)
        self.nc, self.route, self.sorted_x = nc, route, sorted_x
        self.unused = sb("unused", [P, ROUNDS, E])
        self.tab_e = sb("tab_e", [P, FIRST_TILE[-1]], I32)
        self.tab_x = sb("tab_x", [P, FIRST_TILE[-1]], I32)
        self.tab_pad = sb("tab_pad", [P, ROUNDS * E], I32)
        self.zeros = sb("zeros", [P, 1, P])
        self.made = sem("constants_made")
        self.tab = sem("tab")
        self.tab_done = sem("tab_done")
        self.padded = sem("padded")
        self.done = 0
        self.uses = 0

    def scratch(self, buffer):
        most = max(TILES)
        taken = [0]

        def part(n, dt=F32):
            taken[0] += n
            v = buffer[:, taken[0] - n:taken[0]]
            return v.bitcast(dt) if dt != F32 else v

        self.uses += 1
        self.tile_no_i = part(most, I32)
        self.full_i = part(self.KT, I32)
        self.region_i = part(E, I32)
        self.tile_no = part(most)
        self.full = part(self.KT)
        self.region = part(E)
        self.over = part(E * self.KT).rearrange("p (e k) -> p e k", e=E)
        self.tiles_of = part(E)
        self.begins = part(E)
        self.lower = part(E * E).rearrange("p (i j) -> p i j", i=E)
        self.passed = part(most * E).rearrange("p (n e) -> p n e", e=E)
        self.skipped = part(most * E).rearrange("p (n e) -> p n e", e=E)
        self.expert_of = part(most)
        self.row_of = part(most)
        assert taken[0] <= self.SCRATCH

    def constants(self, pool):
        nc = self.nc
        nc.gpsimd.memset(self.zeros[:, :, :], 0.0).then_inc(self.made, 1)
        nc.gpsimd.iota(self.tile_no_i[:, :], pattern=[[1, max(TILES)]], base=0, channel_multiplier=0).then_inc(self.made, 1)
        nc.gpsimd.iota(self.full_i[:, :], pattern=[[CH, self.KT]], base=0, channel_multiplier=0).then_inc(self.made, 1)
        nc.gpsimd.iota(self.region_i[:, :], pattern=[[REG, E]], base=0, channel_multiplier=0).then_inc(self.made, 1)

    def then(self, dve, ins):
        self.done += 1
        ins.then_inc(self.tab, 1)
        dve.wait_ge(self.tab, self.done)

    def converted(self, dve):
        nc = self.nc
        dve.wait_ge(self.made, 4 * self.uses)
        nc.vector.tensor_copy(self.tile_no[:, :], self.tile_no_i[:, :])
        nc.vector.tensor_copy(self.full[:, :], self.full_i[:, :])
        self.then(dve, nc.vector.tensor_copy(self.region[:, :], self.region_i[:, :]))

    def table(self, dve, r):
        self.first_tiles(dve, r)
        self.rows(dve, r)

    def first_tiles(self, dve, r):
        nc = self.nc
        AX = mybir.AxisListType.X
        begins = self.begins
        count = self.route.counts[:, FIRST_GRAPH[r + 1] - 1, :]

        def then(ins):
            self.then(dve, ins)

        then(nc.vector.tensor_tensor(self.over[:, :, :], count.rearrange("p (e o) -> p e o", o=1).to_broadcast([P, E, self.KT]),
                                     self.full[:, :].rearrange("p (o k) -> p o k", o=1).to_broadcast([P, E, self.KT]), ALU.is_gt))
        then(nc.vector.tensor_reduce(self.tiles_of[:, :], self.over[:, :, :], AX, ALU.add))
        mine = self.tiles_of[:, :].rearrange("p (o j) -> p o j", o=1).to_broadcast([P, E, E])
        then(nc.vector.tensor_tensor(self.lower[:, :, :], self.route.before[:, :, :], mine, ALU.mult))
        then(nc.vector.tensor_reduce(begins[:, :], self.lower[:, :, :], AX, ALU.add))
        then(nc.vector.tensor_tensor(begins[:, :], begins[:, :], self.tiles_of[:, :], ALU.add))
        then(nc.vector.tensor_scalar(self.unused[:, r, :], self.tiles_of[:, :], -float(CH), float(REG), ALU.mult, ALU.add))

    def rows(self, dve, r):
        nc = self.nc
        AX = mybir.AxisListType.X
        NT = TILES[r]
        begins, passed, skipped, row_of = self.begins, self.passed, self.skipped, self.row_of
        count = self.route.counts[:, FIRST_GRAPH[r + 1] - 1, :]

        def then(ins):
            self.then(dve, ins)

        nr = self.tile_no[:, 0:NT].rearrange("p (n o) -> p n o", o=1).to_broadcast([P, NT, E])
        er = begins[:, :].rearrange("p (o e) -> p o e", o=1).to_broadcast([P, NT, E])
        ur = self.unused[:, r, :].rearrange("p (o e) -> p o e", o=1).to_broadcast([P, NT, E])
        at = slice(FIRST_TILE[r], FIRST_TILE[r + 1])
        then(nc.vector.tensor_tensor(passed[:, 0:NT, :], nr, er, ALU.is_ge))
        then(nc.vector.tensor_tensor(skipped[:, 0:NT, :], passed[:, 0:NT, :], ur, ALU.mult))
        nc.vector.tensor_reduce(self.expert_of[:, 0:NT], passed[:, 0:NT, :], AX, ALU.add)
        then(nc.vector.tensor_reduce(row_of[:, 0:NT], skipped[:, 0:NT, :], AX, ALU.add))
        then(nc.vector.scalar_tensor_tensor(out=row_of[:, 0:NT], in0=self.tile_no[:, 0:NT], scalar=float(CH), in1=row_of[:, 0:NT],
                                            op0=ALU.mult, op1=ALU.add))
        nc.vector.tensor_scalar(self.tab_x[:, at], row_of[:, 0:NT], float(SPARE), None, ALU.min)
        nc.vector.tensor_scalar(self.tab_e[:, at], self.expert_of[:, 0:NT], float(E - 1), None, ALU.min)
        then(nc.vector.tensor_tensor(self.tab_pad[:, E * r:E * r + E], count, self.region[:, :], ALU.add))
        dve.sem_inc(self.tab_done, 1)

    def spare(self, sp):
        sp.wait_ge(self.made, 1)
        for r in range(ROUNDS):
            sp.dma_start(self.sorted_x[r][SPARE:SPARE + CH, :].rearrange("(p t) d -> p t d", p=P),
                         self.zeros[:, :, :].to_broadcast([P, CT, P])).then_inc(self.padded, 16)

    def pad(self, sp, r, first, end):
        for e in range(first, end):
            row = self.nc.values_load(self.tab_pad[0:1, E * r + e:E * r + e + 1], engines=[mybir.EngineType.SP], min_val=0, max_val=SPARE)
            sp.dma_start(self.sorted_x[r][bass.ds(row, CH), :].rearrange("(p t) d -> p t d", p=P),
                         self.zeros[:, :, :].to_broadcast([P, CT, P])).then_inc(self.padded, 16)


class Weights:

    def __init__(self, nc, sem, W1, W2, stage, first_a):
        assert STG * N == 2 * E * HC * P and T * N == 4 * E * HC * P
        self.nc, self.W1, self.W2 = nc, W1, W2
        rows = stage[:, :, :].rearrange("p s n -> p (s n)").bitcast(F32)
        halves = first_a[:, :, :].rearrange("p t n -> p (t n)")
        n = E * HC * P
        self.w1_raw = rows[:, 0:n].rearrange("p (e h) -> p e h", e=E)
        self.w2_raw = rows[:, n:2 * n].rearrange("p (e c d) -> p e c d", e=E, c=HC)
        self.w1 = halves[:, 0:2 * n].rearrange("p (e w) -> p e w", e=E)
        self.w2 = halves[:, 2 * n:4 * n].rearrange("p (e c s d) -> p e c s d", e=E, c=HC, s=2)
        self.w1_in = sem("w1_in")
        self.w2_in = sem("w2_in")
        self.high = sem("w_high")

    def load(self, sp):
        sp.dma_start(self.w1_raw, self.W1.rearrange("e d h -> d e h")).then_inc(self.w1_in, 16)
        sp.dma_start(self.w2_raw, self.W2.rearrange("e (c h) d -> h e c d", h=P)).then_inc(self.w2_in, 16)

    def split_first(self, dve):
        dve.wait_ge(self.w1_in, 16)
        self.nc.vector.tensor_copy(self.w1[:, :, 0:HC * P], self.w1_raw).then_inc(self.high, 1)
        dve.wait_ge(self.high, 1)
        self.nc.vector.tensor_tensor(self.w1[:, :, HC * P:2 * HC * P], self.w1_raw, f32(self.w1[:, :, 0:HC * P]), ALU.subtract)

    def split_second_high(self, dve):
        dve.wait_ge(self.w2_in, 16)
        self.nc.vector.tensor_copy(self.w2[:, :, :, 0, :], self.w2_raw).then_inc(self.high, 1)

    def split_second_low(self, dve):
        dve.wait_ge(self.high, 2)
        return self.nc.vector.tensor_tensor(self.w2[:, :, :, 1, :], self.w2_raw, f32(self.w2[:, :, :, 0, :]), ALU.subtract)


def graphs(nc, x, adj, weight, w_ih, w_hh, b_ih, b_hh, Wg, bg, bank, x2, ident, stage, first_a, weights, route, plan, sem):
    with ExitStack() as ctx:
        def sb(name, shape, dt=F32):
            return ctx.enter_context(nc.sbuf_tensor(name, shape, dt))

        AG = bank[0:2]
        R, Z, HN, IN = bank[2:6]
        TR = bank[6:8]
        A = [first_a, sb("A1", [P, T, N], R32)]
        hT = [sb("hT0", [P, 2, CH]), route.h_last]
        hT_hi = [sb(f"hT_hi{i}", [P, 2, CH], R32) for i in range(2)]
        hT_lo = [sb(f"hT_lo{i}", [P, 2, CH], R32) for i in range(2)]
        hN_hi = [sb(f"hN_hi{i}", [P, T, P], R32) for i in range(2)]
        hN_lo = [sb(f"hN_lo{i}", [P, T, P], R32) for i in range(2)]
        ag_hi = [sb(f"ag_hi{i}", [P, CH], R32) for i in range(2)]
        ag_lo = [sb(f"ag_lo{i}", [P, CH], R32) for i in range(2)]
        rt = [sb(f"rt{i}", [P, CH]) for i in range(2)]
        zt = [sb(f"zt{i}", [P, CH]) for i in range(2)]
        zh = [sb(f"zh{i}", [P, CH]) for i in range(2)]
        xn = sb("xn", [P, T, P])
        stats = sb("stats", [P, T, 6])
        mv = sb("mv", [P, T, 2])
        veps = sb("veps", [P, T])
        rstd = sb("rstd", [P, T])
        shift = sb("shift", [P, T])
        wi_hi = sb("wi_hi", [P, LAYERS, 3, P], R32)
        wi_lo = sb("wi_lo", [P, LAYERS, 3, P], R32)
        wh_hi = sb("wh_hi", [P, 3, P], R32)
        wh_lo = sb("wh_lo", [P, 3, P], R32)
        bcol = sb("bcol", [P, 6])
        brz = sb("brz", [P, 2])
        wg = route.wg
        bgb = route.bgb
        plan.scratch(xn[:, :, :].rearrange("p t d -> p (t d)"))
        w_raw = rt[0][:, 0:384].rearrange("p (i e) -> p i e", i=3)
        wih_raw = rt[1][:, 0:384].rearrange("p (i e) -> p i e", i=3)
        whh_raw = zt[0][:, 0:384].rearrange("p (i e) -> p i e", i=3)
        wT = zt[1][:, 0:384].rearrange("p (i e) -> p i e", i=3)
        wihT = zh[0][:, 0:384]
        brow = zh[1][0:6, 0:P]
        bg_row = rt[0][0:1, 384:384 + E]
        ones_row = zt[0][0:1, 384:384 + P]

        id_made = sem("id_made")
        sp_passed = sem("sp_passed")
        h_done, tr_full, tr_free, scattered, r_xr, gate = route.h_done, route.tr_full, route.tr_free, route.scattered, route.r_xr, route.gate

        w_loaded = sem("w_loaded")
        w_turned = sem("w_turned")
        w_taken = sem("w_taken")
        w_fused = sem("w_fused")
        w_split = sem("w_split")
        stage_in = [sem(f"stage_in{i}") for i in range(STG)]
        a_made = sem("a_made")
        x_in = [sem(f"x_in{i}") for i in range(3)]
        ln_stats = sem("ln_stats")
        ln_mv = sem("ln_mv")
        ln_veps = sem("ln_veps")
        ln_rstd = sem("ln_rstd")
        ln_xn = sem("ln_xn")
        prep_hi = sem("prep_hi")
        prep_lo = sem("prep_lo")
        prep_t = sem("prep_t")
        bg_full = sem("bg_full")
        tok_hi = sem("tok_hi")
        ag_full = sem("ag_full")
        ag_his = sem("ag_his")
        ag_los = sem("ag_los")
        r_full = sem("r_full")
        z_full = sem("z_full")
        hn_full = sem("hn_full")
        in_full = sem("in_full")
        r_done = sem("r_done")
        z_done = sem("z_done")
        t_done = sem("t_done")
        t2_done = sem("t2_done")
        n_done = sem("n_done")
        v_done = sem("v_done")
        zh_done = sem("zh_done")
        hhi_done = sem("hhi_done")
        hlo_done = sem("hlo_done")

        def chunk_no(it, half, l, c):
            return 12 * it + 6 * half + 2 * l + c

        def tr_no(it, half, k):
            if is_first(it, half):
                return k if k < 6 else k - 2
            if is_last(it, half) and k >= 10:
                k -= 2
            return 24 * it + 12 * half - 4 + k

        def loop(eng, pair):
            pair(0)
            with eng.Fori(1, B // 2 - 1) as it:
                pair(it)
            pair(B // 2 - 1)

        def is_last(it, half):
            return half == 1 and isinstance(it, int) and it == B // 2 - 1

        def prev(it, half):
            return (it, 0) if half else (it - 1, 1)

        def routed(it, half):
            return not (isinstance(it, int) and it == 0)

        def is_first(it, half):
            return half == 0 and isinstance(it, int) and it == 0

        def hidden(l, what, half=None):
            return what[0] if l == 0 else what[1]

        block = ctx.enter_context(nc.Block())

        @block.sync
        def _(sp):
            av = adj.rearrange("b (t p) n -> b t p n", p=P)

            def rows(b, t, n):
                need(sp, a_made, n - STG + 1)
                sp.dma_start(stage[:, t % STG, :], av[b, t, :, :] if isinstance(b, int)
                             else av[bass.ds(b, 1), t, :, :].rearrange("o p n -> (o p) n")).then_inc(stage_in[t % STG], 16)

            for t in range(T):
                rows(0, t, t)

            def pair(it):
                for half in range(2):
                    if not is_last(it, half):
                        nxt = 2 * it + half + 1
                        for t in range(T):
                            rows(nxt, t, 8 * nxt + t)
                        if is_first(it, half):
                            sp.dma_start(x2[:, 2 * T:B * T, :], x.rearrange("b (t p) d -> p (b t) d", p=P)[:, 2 * T:B * T, :]).then_inc(x_in[2], 16)

            loop(sp, pair)
            sp.wait_ge(a_made, 8 * B)
            weights.load(sp)
            plan.spare(sp)
            sp.wait_ge(plan.tab_done, 1)
            sp.sem_inc(sp_passed, 1)
            sp.wait_ge(scattered, 16 * TOP * T * FIRST_GRAPH[1])
            sp.sem_inc(sp_passed, 1)
            plan.pad(sp, 0, 0, E)
            sp.wait_ge(plan.padded, 16 * (ROUNDS + E))

        @block.gpsimd
        def _(pool):
            nc.gpsimd.memset(route.mhalf[:, :], -0.5).then_inc(id_made, 1)
            nc.gpsimd.memset(ident[:, :], 0.0).then_inc(id_made, 1)
            pool.wait_ge(id_made, 2)
            nc.gpsimd.affine_select(out=ident[:, :], in_=ident[:, :], compare_op=ALU.not_equal, fill=1.0,
                                    base=0, pattern=[[-1, P]], channel_multiplier=1).then_inc(id_made, 1)

            nc.gpsimd.memset(ones_row[:, :], 1.0).then_inc(id_made, 1)
            nc.gpsimd.memset(route.ones[:, :], 1.0).then_inc(id_made, 1)
            nc.gpsimd.memset(route.earlier[:, :], 1.0).then_inc(id_made, 1)
            nc.gpsimd.memset(route.before[:, :, :], 1.0).then_inc(id_made, 1)
            nc.gpsimd.memset(route.offset[:, :], 0.0).then_inc(id_made, 1)
            nc.gpsimd.memset(route.keep_count[:, :], 1.0).then_inc(id_made, 1)
            pool.wait_ge(id_made, 9)
            nc.gpsimd.affine_select(out=route.earlier[:, :], in_=route.earlier[:, :], compare_op=ALU.is_gt, fill=0.0,
                                    base=0, pattern=[[1, P]], channel_multiplier=-1).then_inc(id_made, 1)
            nc.gpsimd.affine_select(out=route.before[:, :, :], in_=route.before[:, :, :], compare_op=ALU.is_gt, fill=0.0,
                                    base=0, pattern=[[1, E], [-1, E]], channel_multiplier=0).then_inc(id_made, 1)
            for e in range(E):
                ins = nc.gpsimd.memset(route.region[:, :, e], float(e * REG + 1))
            for r in range(ROUNDS):
                ins = nc.gpsimd.memset(route.keep_count[:, FIRST_GRAPH[r]:FIRST_GRAPH[r] + 1], 0.0)
            nc.gpsimd.memset(route.sel_bf[:, T, :], 0.0)
            ins.then_inc(id_made, 1)

            def input_scale(nb):
                pool.wait_ge(ln_veps, nb + 1)
                nc.gpsimd.tensor_tensor(rstd[:, :], veps[:, :], route.mhalf[:, :], ALU.pow).then_inc(ln_rstd, 1)
                pool.wait_ge(ln_rstd, 2 * nb + 1)
                nc.gpsimd.tensor_tensor(shift[:, :], shift[:, :], rstd[:, :], ALU.mult).then_inc(ln_rstd, 1)

            def input_lo(nb):
                pool.wait_ge(prep_hi, nb + 1)
                need(pool, ag_full, 6 * (nb - 1) + 2)
                nc.gpsimd.tensor_tensor(hN_lo[0][:, :, :], xn[:, :, :], f32(hN_hi[0][:, :, :]),
                                        ALU.subtract).then_inc(prep_lo, 1)

            input_scale(0)
            input_lo(0)

            def keep(it, half, l, c):
                n = chunk_no(it, half, l, c)
                pool.wait_ge(z_done, n + 1)
                if l == 0:
                    pool.wait_ge(prep_t, 4 * (2 * it + half) + 4)
                else:
                    pool.wait_ge(h_done, n - 1)
                need(pool, h_done, n - 1)
                nc.gpsimd.tensor_tensor(zh[c][:, :], zt[c][:, :], hidden(l, hT)[:, c, :],
                                        ALU.mult).then_inc(zh_done, 1)

            def pair(it):
                for half in range(2):
                    more = not is_last(it, half)
                    nb = 2 * it + half + 1
                    for l in range(LAYERS):
                        for c in range(2):
                            keep(it, half, l, c)
                            if l == 2 and c == 0 and more:
                                input_lo(nb)
                            if l == 0 and c == 0 and not more:
                                plan.constants(pool)
                        if l == 1 and more:
                            input_scale(nb)
                        if routed(it, half):
                            n = 3 if more else 4
                            route.scatter(pool, 2 * it + half - 2, half, min(n * l, T), min(n * l + n, T))
                        if l == 0 and not is_first(it, half):
                            route.scale(pool, 2 * it + half - 1)

            loop(pool, pair)

        @block.scalar
        def _(act):
            act.dma_start(x2[:, 0:T, :], x.rearrange("b (t p) d -> b p t d", p=P)[0, :, :, :]).then_inc(x_in[0], 16)
            act.dma_start(w_raw, weight.rearrange("i d e -> d i e")).then_inc(w_loaded, 16)
            act.dma_start(wih_raw, w_ih.rearrange("(i j) e -> j i e", j=P)).then_inc(w_loaded, 16)
            act.dma_start(whh_raw, w_hh.rearrange("(i j) e -> j i e", j=P)).then_inc(w_loaded, 16)
            act.dma_start(brow[0:3, :], b_ih.rearrange("(i j) -> i j", j=P)).then_inc(w_loaded, 16)
            act.dma_start(brow[3:6, :], b_hh.rearrange("(i j) -> i j", j=P)).then_inc(w_loaded, 16)
            act.dma_start(wg[:, :], Wg).then_inc(w_loaded, 16)
            act.dma_start(bg_row[:, :], bg.rearrange("(o e) -> o e", o=1)).then_inc(w_loaded, 16)
            act.dma_start(x2[:, T:2 * T, :], x.rearrange("b (t p) d -> b p t d", p=P)[1, :, :, :]).then_inc(x_in[1], 16)

            def input_hi(nb):
                act.wait_ge(ln_xn, nb + 1)
                need(act, ag_full, 6 * (nb - 1) + 2)
                nc.scalar.activation(hN_hi[0][:, :, :], xn[:, :, :], ACT.Copy).then_inc(prep_hi, 1)

            def input_turned(nb, c, tr, k):
                act.wait_ge(tr_full, tr + 1)
                need(act, zh_done, 6 * (nb - 1) + c + 1)
                need(act, hn_full, 6 * (nb - 1) + c + 1)
                nc.scalar.activation(hT[0][:, c, :], TR[k % 2][:, :], ACT.Copy).then_inc(prep_t, 1)
                nc.scalar.activation(hT_hi[0][:, c, :], TR[k % 2][:, :], ACT.Copy).then_inc(prep_t, 1)

            def input_apply(nb):
                act.wait_ge(ln_rstd, 2 * nb + 2)
                need(act, prep_lo, nb)
                need(act, tr_full, (0, 2, 8)[nb] if isinstance(nb, int) and nb < 3 else 12 * nb - 18)
                route.normalise(nb, xn, rstd, shift, ln_xn)

            input_apply(0)
            input_hi(0)
            for c in range(2):
                input_turned(0, c, c, c)

            def node_major_hi(it, half, l, c):
                n = chunk_no(it, half, l, c)
                k = 2 + 2 * l + c
                act.wait_ge(tr_full, tr_no(it, half, k) + 1)
                if c == 0:
                    act.wait_ge(ag_full, n + 2)
                nc.scalar.activation(hN_hi[1][:, CT * c:CT * c + CT, :], TR[k % 2][:, :].rearrange("p (t d) -> p t d", t=CT),
                                     ACT.Copy).then_inc(tok_hi, 1)

            def pair(it):
                for half in range(2):
                    more = not is_last(it, half)
                    nb = 2 * it + half + 1
                    for l in range(LAYERS):
                        for c in range(2):
                            n = chunk_no(it, half, l, c)
                            act.wait_ge(ag_full, n + 1)
                            need(act, in_full, n - 1)
                            nc.scalar.activation(ag_hi[c][:, :], AG[c][:, :], ACT.Copy).then_inc(ag_his, 1)
                            if l == 2 and c == 0 and not is_first(it, half):
                                for k in range(2):
                                    route.turned(act, nb - 2, k, TR[k], tr_no(it, half, 6 + k))
                        for c in range(2):
                            n = chunk_no(it, half, l, c)
                            act.wait_ge(r_full, n + 1)
                            need(act, h_done, n - 1)
                            if is_first(it, half) and l == 0:
                                act.wait_ge(w_split, 4)
                            nc.scalar.activation(rt[c][:, :], R[:, :], ACT.Sigmoid, bias=brz[:, 0:1]).then_inc(r_done, 1)
                            act.wait_ge(z_full, n + 1)
                            nc.scalar.activation(zt[c][:, :], Z[:, :], ACT.Sigmoid, bias=brz[:, 1:2]).then_inc(z_done, 1)
                            if l == 2 and more:
                                input_turned(nb, c, tr_no(it, half, 8 + c), 8 + c)
                            if c == 1 and l < 2:
                                node_major_hi(it, half, l, 0)
                            act.wait_ge(t2_done, n + 1)
                            nc.scalar.activation(rt[c][:, :], rt[c][:, :], ACT.Tanh, bias=bcol[:, 2:3]).then_inc(n_done, 1)
                            if l == 2 and c == 0 and more:
                                input_hi(nb)
                        if l == 1 and not is_first(it, half):
                            route.apply(act, nb - 2, 1 - half)
                        if l < 2:
                            node_major_hi(it, half, l, 1)
                        if l == 1 and more:
                            input_apply(nb)
            loop(act, pair)
        @block.vector
        def _(dve):
            def input_norm(nb):
                dve.wait_ge(x_in[nb if isinstance(nb, int) and nb < 2 else 2], 16)
                need(dve, ln_xn, nb)
                route.moments(dve, nb, stats, mv, veps, shift, ln_stats, ln_mv, ln_veps)

            def convert(half, t, nb):
                dve.wait_ge(stage_in[t % STG], 16 * (2 * nb + t // STG + 1))
                if t == 0:
                    need(dve, ag_full, 6 * (nb - 1))
                nc.vector.tensor_scalar(A[half][:, t, :], stage[:, t % STG, :], 0, None,
                                        ALU.not_equal).then_inc(a_made, 1)

            def input_turned_lo(nb, c, k):
                dve.wait_ge(prep_t, 4 * nb + 2 * c + 2)
                need(dve, hn_full, 6 * (nb - 1) + c + 1)
                nc.vector.tensor_tensor(hT_lo[0][:, c, :], TR[k % 2][:, :], f32(hT_hi[0][:, c, :]),
                                        ALU.subtract).then_inc(tr_free, 1)

            input_norm(0)
            for t in range(STG):
                convert(0, t, 0)
            dve.wait_ge(w_turned, 4)
            nc.vector.tensor_copy(wT, AG[0][:, 0:384].rearrange("p (i e) -> p i e", i=3)).then_inc(w_taken, 1)
            nc.vector.tensor_copy(wihT, AG[1][:, 0:384]).then_inc(w_taken, 1)
            nc.vector.tensor_copy(bcol[:, :], Z[:, 0:6]).then_inc(w_taken, 1)
            nc.vector.tensor_copy(wh_hi[:, :, :], R[:, 0:384].rearrange("p (i e) -> p i e", i=3)).then_inc(w_taken, 1)
            dve.wait_ge(w_taken, 4)
            nc.vector.tensor_tensor(brz[:, :], bcol[:, 0:2], bcol[:, 3:5], ALU.add).then_inc(w_split, 1)
            nc.vector.tensor_tensor(wh_lo[:, :, :], R[:, 0:384].rearrange("p (i e) -> p i e", i=3),
                                    f32(wh_hi[:, :, :]), ALU.subtract).then_inc(w_split, 1)
            dve.wait_ge(bg_full, 1)
            nc.vector.tensor_copy(bgb[:, :], TR[0][:, 0:E]).then_inc(w_taken, 1)
            for t in range(STG, T - 2):
                convert(0, t, 0)
            fused = [HN, IN, AG[0]]
            dve.wait_ge(w_fused, 1)
            for l in range(LAYERS):
                src = fused[l][:, 0:384].rearrange("p (i e) -> p i e", i=3)
                ins = nc.vector.tensor_copy(wi_hi[:, l, :, :], src)
            ins.then_inc(w_split, 1)
            dve.wait_ge(w_split, 3)
            for l in range(LAYERS):
                src = fused[l][:, 0:384].rearrange("p (i e) -> p i e", i=3)
                ins = nc.vector.tensor_tensor(wi_lo[:, l, :, :], src, f32(wi_hi[:, l, :, :]), ALU.subtract)
            ins.then_inc(w_split, 1)
            for c in range(2):
                input_turned_lo(0, c, c)
            for t in range(T - 2, T):
                convert(0, t, 0)

            def node_major_lo(it, half, l, c):
                n = chunk_no(it, half, l, c)
                k = 2 + 2 * l + c
                dve.wait_ge(tok_hi, 8 * it + 4 * half + 2 * l + c + 1)
                nc.vector.tensor_tensor(hN_lo[1][:, CT * c:CT * c + CT, :], TR[k % 2][:, :].rearrange("p (t d) -> p t d", t=CT),
                                        f32(hN_hi[1][:, CT * c:CT * c + CT, :]), ALU.subtract).then_inc(tr_free, 1)

            def converts(half, nb, more, *tiles):
                if more:
                    for t in tiles:
                        convert((half + 1) % 2, t, nb)

            def pair(it):
                for half in range(2):
                    more = not is_last(it, half)
                    nb = 2 * it + half + 1
                    for l in range(LAYERS):
                        if l == 0 and more:
                            input_norm(nb)
                        if l == 0 and routed(it, half):
                            route.places(dve, nb - 3, TR[1], tr_no(*prev(it, half), 11))
                        for c in range(2):
                            n = chunk_no(it, half, l, c)
                            dve.wait_ge(ag_his, n + 1)
                            nc.vector.tensor_tensor(ag_lo[c][:, :], AG[c][:, :], f32(ag_hi[c][:, :]),
                                                    ALU.subtract).then_inc(ag_los, 1)
                        if l == 0 and not is_first(it, half):
                            for c in range(2):
                                route.residual(dve, nb - 2, c, TR[c], tr_no(it, half, c))
                        if l == 2:
                            converts(half, nb, more, 6)
                            if not more:
                                weights.split_second_high(dve)
                        for c in range(2):
                            n = chunk_no(it, half, l, c)
                            dve.wait_ge(r_done, n + 1)
                            dve.wait_ge(hn_full, n + 1)
                            nc.vector.scalar_tensor_tensor(out=rt[c][:, :], in0=HN[:, :], scalar=bcol[:, 5:6],
                                                           in1=rt[c][:, :], op0=ALU.add, op1=ALU.mult).then_inc(t_done, 1)
                            dve.wait_ge(t_done, n + 1)
                            dve.wait_ge(in_full, n + 1)
                            nc.vector.tensor_tensor(rt[c][:, :], IN[:, :], rt[c][:, :], ALU.add).then_inc(t2_done, 1)
                            if c == 1 and l < 2:
                                node_major_lo(it, half, l, 0)
                            if l == 2 and more:
                                input_turned_lo(nb, c, c)
                            if l == 0 and c == 0:
                                converts(half, nb, more, 0)
                            if l == 1 and c == 0 and not more:
                                plan.rows(dve, 0)
                            dve.wait_ge(n_done, n + 1)
                            dve.wait_ge(z_done, n + 1)
                            nc.vector.scalar_tensor_tensor(out=rt[c][:, :], in0=zt[c][:, :], scalar=1.0, in1=rt[c][:, :],
                                                           op0=ALU.subtract, op1=ALU.mult).then_inc(v_done, 1)
                            dve.wait_ge(v_done, n + 1)
                            dve.wait_ge(zh_done, n + 1)
                            nc.vector.tensor_tensor(hT[1][:, c, :], zh[c][:, :], rt[c][:, :],
                                                    ALU.subtract).then_inc(h_done, 1)
                            if l < 2:
                                dve.wait_ge(h_done, n + 1)
                                nc.vector.tensor_copy(hT_hi[1][:, c, :], hT[1][:, c, :]).then_inc(hhi_done, 1)
                                dve.wait_ge(hhi_done, 8 * it + 4 * half + 2 * l + c + 1)
                                nc.vector.tensor_tensor(hT_lo[1][:, c, :], hT[1][:, c, :], f32(hT_hi[1][:, c, :]),
                                                        ALU.subtract).then_inc(hlo_done, 1)
                            if l == 2 and c == 0:
                                converts(half, nb, more, 7)
                        if l < 2:
                            node_major_lo(it, half, l, 1)
                        if l == 0 and not is_first(it, half):
                            route.norm(dve, nb - 2, tr_no(it, half, 1))
                        if l < 2:
                            converts(half, nb, more, *((1,), (2, 3, 4, 5))[l])
                        if l == 0 and not more:
                            plan.converted(dve)
                            plan.first_tiles(dve, 0)
                        if l == 1 and not more:
                            weights.split_first(dve)
                        if l == 2 and more and not is_first(it, half):
                            route.gates(dve, nb - 2, TR[0], tr_no(it, half, 10))

            loop(dve, pair)
        @block.tensor
        def _(pe):
            pe.wait_ge(id_made, 3)
            pe.wait_ge(w_loaded, 16 * 7)
            for dst, src in ((AG[0], w_raw), (AG[1], wih_raw), (R, whh_raw)):
                for i in range(3):
                    ins = nc.tensor.transpose(dst[:, P * i:P * i + P], src[:, i, :], ident[:, :])
                ins.then_inc(w_turned, 1)
            nc.tensor.transpose(Z[:, 0:6], brow, ident[0:6, 0:6]).then_inc(w_turned, 1)
            pe.wait_ge(id_made, 12)
            nc.tensor.matmul(TR[0][:, 0:E], ones_row[:, :], bg_row[:, :], start=True, stop=True).then_inc(bg_full, 1)
            pe.wait_ge(w_taken, 2)
            for l, dst in enumerate((HN, IN, AG[0])):
                ins = nc.tensor.matmul(dst[:, 0:384], wT[:, l, :], wihT, start=True, stop=True)
            ins.then_inc(w_fused, 1)

            def input_turn(nb, c, tr, k):
                pe.wait_ge(ln_xn, nb + 1)
                need(pe, tr_free, tr - 1)
                for t in range(CT):
                    ins = nc.tensor.transpose(TR[k % 2][:, P * t:P * t + P], xn[:, CT * c + t, :], ident[:, :])
                ins.then_inc(tr_full, 1)

            def aggregate(it, half, l, c, part):
                n = chunk_no(it, half, l, 0)
                g = half
                for t in range(CT * part, CT * part + CT):
                    for h in (hidden(l, hN_hi), hidden(l, hN_lo)):
                        ins = nc.tensor.matmul(AG[c][:, :], h[:, t, :], A[g][:, t, CH * c:CH * c + CH],
                                               start=(t == 0 and h is hidden(l, hN_hi)),
                                               stop=(t == T - 1 and h is hidden(l, hN_lo)))
                if part == 1:
                    ins.then_inc(ag_full, 1)

            def products(dst, w_hi, w_lo, r_hi, r_lo, start, stop):
                for i, (w, r) in enumerate(((w_hi, r_hi), (w_hi, r_lo), (w_lo, r_hi))):
                    ins = nc.tensor.matmul(dst[:, :], w, r, start=(start and i == 0), stop=(stop and i == 2))
                return ins

            def from_h(it, half, l, c):
                n = chunk_no(it, half, l, c)
                b = 2 * it + half
                if l == 0:
                    pe.wait_ge(prep_t, 4 * b + 2 * c + 2)
                    pe.wait_ge(tr_free, c + 1 if is_first(it, half) else tr_no(*prev(it, half), 8 + c) + 1)
                else:
                    pe.wait_ge(hlo_done, 8 * it + 4 * half + 2 * (l - 1) + c + 1)
                r_hi, r_lo = hidden(l, hT_hi)[:, c, :], hidden(l, hT_lo)[:, c, :]
                need(pe, r_done, n)
                products(R, wh_hi[:, 0, :], wh_lo[:, 0, :], r_hi, r_lo, True, False)
                need(pe, z_done, n)
                products(Z, wh_hi[:, 1, :], wh_lo[:, 1, :], r_hi, r_lo, True, False)
                need(pe, t_done, n)
                products(HN, wh_hi[:, 2, :], wh_lo[:, 2, :], r_hi, r_lo, True, True).then_inc(hn_full, 1)

            def from_ag(it, half, l, c):
                n = chunk_no(it, half, l, c)
                pe.wait_ge(ag_los, n + 1)
                r_hi, r_lo = ag_hi[c][:, :], ag_lo[c][:, :]
                products(R, wi_hi[:, l, 0, :], wi_lo[:, l, 0, :], r_hi, r_lo, False, True).then_inc(r_full, 1)
                products(Z, wi_hi[:, l, 1, :], wi_lo[:, l, 1, :], r_hi, r_lo, False, True).then_inc(z_full, 1)
                need(pe, t2_done, n)
                products(IN, wi_hi[:, l, 2, :], wi_lo[:, l, 2, :], r_hi, r_lo, True, True).then_inc(in_full, 1)

            pe.wait_ge(w_taken, 5)
            for c in range(2):
                input_turn(0, c, c, c)
            pe.wait_ge(w_split, 4)

            def pair(it):
                for half in range(2):
                    b = 2 * it + half
                    for l in range(LAYERS):
                        n = chunk_no(it, half, l, 0)
                        if l > 0:
                            route.output_turn(pe, n - 2, 0, TR[0], tr_no(it, half, 2 * l))
                        from_h(it, half, l, 0)
                        if l == 0:
                            pe.wait_ge(prep_lo, b + 1)
                            pe.wait_ge(a_made, 8 * b + CT)
                        else:
                            pe.wait_ge(tr_free, tr_no(it, half, 2 * l) + 1)
                        need(pe, ag_los, n - 1)
                        aggregate(it, half, l, 0, 0)
                        if l > 0:
                            route.output_turn(pe, n - 1, 1, TR[1], tr_no(it, half, 2 * l + 1))
                        need(pe, ag_los, n)
                        aggregate(it, half, l, 1, 0)
                        if l == 0 and routed(it, half):
                            route.count(pe, b - 2, TR[1], tr_no(*prev(it, half), 11))
                        if l == 0:
                            pe.wait_ge(a_made, 8 * b + T)
                        else:
                            pe.wait_ge(tr_free, tr_no(it, half, 2 * l + 1) + 1)
                        aggregate(it, half, l, 0, 1)
                        if l == 2 and not is_first(it, half):
                            for c in range(2):
                                route.result_turn(pe, b - 1, 1 - half, c, TR[c], tr_no(it, half, 6 + c))
                        aggregate(it, half, l, 1, 1)
                        if l == 0 and not is_first(it, half):
                            for c in range(2):
                                route.output_turn(pe, n - 2 + c, c, TR[c], tr_no(it, half, c))
                        if l == 2 and not is_last(it, half):
                            input_turn(b + 1, 0, tr_no(it, half, 8), 0)
                        from_ag(it, half, l, 0)
                        if l == 2 and not is_last(it, half):
                            input_turn(b + 1, 1, tr_no(it, half, 9), 1)
                        from_h(it, half, l, 1)
                        if l == 2 and not is_first(it, half):
                            route.scores(pe, b - 1, TR[0], tr_no(it, half, 10), is_last(it, half))
                        from_ag(it, half, l, 1)

            loop(pe, pair)


def experts(nc, weights, b1, b2, out, bank, x2, ident, sorted_x, sorted_y, route, plan, sem):
    M = FIRST_TILE[-1]
    WW = 2 * HC * P
    LAST = route.LAST
    tab_e, tab_x, unused = plan.tab_e, plan.tab_x, plan.unused
    with ExitStack() as ctx:
        def sb(name, shape, dt=F32):
            return ctx.enter_context(nc.sbuf_tensor(name, shape, dt))

        U = bank[0:4]
        XT = bank[4]
        Y = bank[5:7]
        TR = bank[7]
        plan_scratch = sb("plan_scratch", [P, plan.SCRATCH])
        plan.scratch(plan_scratch)
        b_raw = sb("b_raw", [2 * E, P])
        b2_raw = sb("b2_raw", [2, E, P])
        w1_all, w2_all = weights.w1, weights.w2
        b1_all = sb("b1_all", [P, E, HC])
        b2_hi = sb("b2_hi", [2, E, P], R32)
        b2_all = sb("b2_all", [2, E, 2, P], R32)
        b2_zero = sb("b2_zero", [2, E, P])
        is_low = sb("is_low", [2, 1])
        ones_f = sb("ones_f", [2, P])
        ones_r = sb("ones_r", [2, P], R32)
        w1 = [sb(f"w1_{i}", [P, WW], R32) for i in range(2)]
        bias1 = [sb(f"bias1_{i}", [P, HC]) for i in range(2)]
        row_in = sb("row_in", [P, B * T * TOP])
        row_out = sb("row_out", [P, B * T * TOP])
        row_less = sb("row_less", [P, B * T * TOP])
        y_rows = sb("y_rows", [P, B, T, TOP], I32)
        xg = [sb(f"xg{i}", [P, CT, P]) for i in range(2)]
        xT_hi = [sb(f"xT_hi{i}", [P, CH], R32) for i in range(2)]
        xT_lo = [sb(f"xT_lo{i}", [P, CH], R32) for i in range(2)]
        g = [[sb(f"g{i}{c}", [P, CH]) for c in range(HC)] for i in range(2)]
        g_hi = [[sb(f"g_hi{i}{c}", [P, CH], R32) for c in range(HC)] for i in range(2)]
        g_lo = [[sb(f"g_lo{i}{c}", [P, CH], R32) for c in range(HC)] for i in range(2)]
        ylo = [sb(f"ylo{h}", [P, 2, P]) for h in range(2)]
        yo = [sb(f"yo{i}", [P, CT, P]) for i in range(2)]
        got = [sb(f"got{i}", [P, T, TOP, P]) for i in range(2)]
        fo = [sb(f"fo{i}", [P, T, P]) for i in range(2)]

        b_in = sem("b_in")
        made = sem("made")
        b_turned = sem("b_turned")
        b_taken = sem("b_taken")
        w_ready = sem("w_ready")
        row_step = sem("row_step")
        y_rows_made = sem("y_rows_made")
        x_in = [sem(f"xg_in{i}") for i in range(2)]
        xt_full = sem("xt_full")
        x_hi = sem("x_hi")
        x_lo = sem("x_lo")
        w1_set = sem("w1_set")
        u_full = sem("u_full")
        g_made = sem("g_made")
        g_his = [sem(f"g_his{c}") for c in range(HC)]
        g_los = sem("g_los")
        down = sem("down")
        y_low = sem("y_low")
        yo_made = sem("yo_made")
        y_stored = [sem(f"y_stored{i}") for i in range(2)]
        got_in = [sem(f"got_in{i}") for i in range(2)]
        summed = sem("summed")
        fo_made = sem("fo_made")
        out_stored = [sem(f"out_stored{i}") for i in range(2)]
        e_passed = sem("e_passed")

        block = ctx.enter_context(nc.Block())

        ROUTED = 16
        PART_TILES = (3, 3, 2)
        PARTS = len(PART_TILES)
        PERIOD = PARTS + 1
        SUM_AT = (FIRST_TILE[1] + 6) // 2 * 2
        SUMS_IN_STEPS = (M + 1 - SUM_AT) // PERIOD
        LOOP_END = (M - 4) // 2 * 2

        def of(table, m):
            return table[0:1, m:m + 1] if isinstance(m, int) else table[0:1, bass.ds(m, 1)]

        def there(m):
            return not isinstance(m, int) or 0 <= m < M

        def evens(m, p):
            return 2 * (m // 2) if not isinstance(m, int) else m - p

        def loop(eng, step, summing=None):
            end = LOOP_END if summing is None else SUM_AT
            for n in range(-3, ROUTED):
                step(n, n % 2)
            with eng.Fori(ROUTED // 2, end // 2) as i:
                for k in range(2):
                    step(2 * i + k, k)
            for n in range(end, M + 1):
                step(n, n % 2)
                q, part = divmod(n - SUM_AT, PERIOD)
                if summing is not None and q < SUMS_IN_STEPS:
                    summing(q, part)
            if summing is not None:
                for q in range(SUMS_IN_STEPS, B):
                    for part in range(PERIOD):
                        summing(q, part)

        @block.sync
        def _(sp):
            sp.dma_start(b_raw[:, :], b1.rearrange("e (c j) -> (e c) j", j=P)).then_inc(b_in, 16)
            for i in range(2):
                sp.dma_start(b2_raw[i:i + 1, :, :], b2.rearrange("(o e) d -> o e d", o=1)).then_inc(b_in, 16)

            def step(n, k, r_in, r_out):
                m = n + 3
                if there(m):
                    p = 1 - k
                    need(sp, xt_full, m - 1)
                    sp.sem_inc(e_passed, 1)
                    row = nc.values_load(of(tab_x, m), engines=[mybir.EngineType.SP], min_val=0, max_val=SPARE)
                    sp.dma_start(xg[p][:, :, :], sorted_x[r_in][bass.ds(row, CH), :].rearrange("(p t) d -> p t d", p=P)).then_inc(x_in[p], 16)
                m = n - 1
                if there(m):
                    p = 1 - k
                    sp.wait_ge(yo_made, 2 * m + 2)
                    at = m - FIRST_TILE[r_out]
                    dst = sorted_y[r_out][CH * at:CH * at + CH, :] if isinstance(m, int) else sorted_y[r_out][bass.ds(CH * at, CH), :]
                    sp.dma_start(dst.rearrange("(p t) d -> p t d", p=P), yo[p][:, :, :]).then_inc(y_stored[p], 16)

            for n in range(-3, ROUTED):
                step(n, n % 2, 0, 0)
            begin = ROUTED
            for r in range(1, ROUNDS):
                first = FIRST_TILE[r]
                pad_at = (first - 8) // 2 * 2
                if begin < pad_at:
                    with sp.Fori(begin // 2, pad_at // 2) as i:
                        for k in range(2):
                            step(2 * i + k, k, r - 1, r - 1)
                sp.wait_ge(plan.tab_done, r + 1)
                sp.sem_inc(e_passed, 1)
                sp.wait_ge(route.scattered, 16 * TOP * T * FIRST_GRAPH[r + 1])
                sp.sem_inc(e_passed, 1)
                end = (first + 3) // 2 * 2
                for n in range(pad_at, end):
                    if n < pad_at + E // 2:
                        plan.pad(sp, r, 2 * (n - pad_at), 2 * (n - pad_at) + 2)
                    if n == first - 3:
                        sp.wait_ge(plan.padded, 16 * (ROUNDS + E * (r + 1)))
                    step(n, n % 2, r if n + 3 >= first else r - 1, r if n - 1 >= first else r - 1)
                begin = end
            with sp.Fori(begin // 2, LOOP_END // 2) as i:
                for k in range(2):
                    step(2 * i + k, k, ROUNDS - 1, ROUNDS - 1)
            for n in range(LOOP_END, M + 1):
                step(n, n % 2, ROUNDS - 1, ROUNDS - 1)

        @block.gpsimd
        def _(pool):
            plan.constants(pool)
            nc.gpsimd.memset(ones_f[:, :], 1.0).then_inc(made, 1)
            nc.gpsimd.memset(is_low[:, :], -1.0).then_inc(made, 1)
            nc.gpsimd.memset(b2_zero[:, :, :], 0.0).then_inc(made, 1)
            pool.wait_ge(made, 3)
            nc.gpsimd.memset(is_low[0:1, :], 0.0).then_inc(made, 1)
            route.scatter(pool, B - 2, 0, 0, 4)
            route.scale(pool, B - 1)
            route.scatter(pool, B - 2, 0, 4, T)
            route.scatter(pool, B - 1, 1, 0, T)
            def result_rows(r):
                w = T * TOP
                at = slice(w * FIRST_GRAPH[r], w * FIRST_GRAPH[r + 1])
                n = 2 * E * r
                pool.wait_ge(plan.tab_done, r + 1)
                nc.gpsimd.tensor_copy(row_in[:, at], route.slots[:, at]).then_inc(row_step, 1)
                nc.gpsimd.tensor_copy(row_out[:, at], route.slots[:, at]).then_inc(row_step, 1)
                for e in range(1, E):
                    pool.wait_ge(row_step, n + 2 * e)
                    nc.gpsimd.tensor_scalar(row_less[:, at], row_in[:, at], float(e * REG), unused[:, r, e - 1:e],
                                            ALU.is_ge, ALU.mult).then_inc(row_step, 1)
                    pool.wait_ge(row_step, n + 2 * e + 1)
                    nc.gpsimd.tensor_tensor(row_out[:, at], row_out[:, at], row_less[:, at], ALU.subtract).then_inc(row_step, 1)
                pool.wait_ge(row_step, n + 2 * E)
                nc.gpsimd.tensor_copy(y_rows[:, FIRST_GRAPH[r]:FIRST_GRAPH[r + 1], :, :].rearrange("p b t k -> p (b t k)"),
                                      row_out[:, at]).then_inc(y_rows_made, 1)

            for r in range(ROUNDS):
                result_rows(r)
            for q in range(B):
                p = q % 2
                r = round_of(q)
                if q == FIRST_GRAPH[r]:
                    pool.wait_ge(y_rows_made, r + 1)
                    for k in range(2):
                        pool.wait_ge(y_stored[k], 16 * ((FIRST_TILE[r + 1] + 1 - k) // 2))
                    pool.sem_inc(route.pool_passed, 1)
                need(pool, summed, PARTS * (q - 1))
                pool.sem_inc(route.pool_passed, 1)
                for t in range(T):
                    for j in range(TOP):
                        nc.gpsimd.indirect_dma_start(
                            out=got[p][:, t, j, :], out_offset=None, in_=sorted_y[r],
                            in_offset=bass.IndirectOffsetOnAxis(ap=y_rows[:, q, t, j:j + 1].bitcast(U32), axis=0)).then_inc(got_in[p], 16)

        @block.scalar
        def _(act):
            def step(n, k):
                m = n - 1
                if there(m):
                    for h in range(2):
                        act.wait_ge(down, 2 * m + h + 1)
                        need(act, yo_made, 2 * m + h - 1)
                        nc.scalar.activation(ylo[h][:, :, :], Y[h][:, :].rearrange("p (t s d) -> p t s d", t=2, s=2)[:, :, 1, :],
                                             ACT.Copy).then_inc(y_low, 1)
                m = n + 2
                if there(m):
                    act.wait_ge(xt_full, m + 1)
                    need(act, u_full, 2 * m - 2)
                    nc.scalar.activation(xT_hi[k][:, :], XT[:, :], ACT.Copy).then_inc(x_hi, 1)
                m = n + 1
                if there(m):
                    p = 1 - k
                    for c in range(HC):
                        act.wait_ge(u_full, 2 * m + c + 1)
                        need(act, g_los, 2 * m + c - 3)
                        nc.scalar.activation(g[p][c][:, :], U[2 * p + c][:, :], ACT.Gelu, bias=bias1[p][:, c:c + 1]).then_inc(g_made, 1)
                    need(act, down, 2 * m - 2)
                    for c in range(HC):
                        act.wait_ge(g_made, 2 * m + c + 1)
                        nc.scalar.activation(g_hi[p][c][:, :], g[p][c][:, :], ACT.Copy).then_inc(g_his[c], 1)
                if isinstance(n, int):
                    if n == 2:
                        route.apply(act, B - 1, 1)
                    if n in (4, 6):
                        route.turned(act, B - 1, n // 2 - 2, TR, LAST + n // 2)

            def store(q, part):
                if part == PARTS:
                    act.wait_ge(fo_made, PARTS * q + PARTS)
                    act.dma_start(out.rearrange("b (t p) d -> b p t d", p=P)[q, :, :, :], fo[q % 2][:, :, :]).then_inc(out_stored[q % 2], 16)

            loop(act, step, store)
            for p in range(2):
                act.wait_ge(out_stored[p], 16 * B // 2)

        @block.vector
        def _(dve):
            route.gates(dve, B - 2, bank[6], LAST - 2)
            route.places(dve, B - 2, TR, LAST - 1)
            dve.wait_ge(b_turned, 1)
            nc.vector.tensor_copy(b1_all[:, :, :].rearrange("p e c -> p (e c)"), XT[:, 0:2 * E]).then_inc(b_taken, 1)
            dve.wait_ge(made, 4)
            dve.wait_ge(b_in, 48)
            nc.vector.tensor_copy(ones_r[:, :], ones_f[:, :])
            nc.vector.tensor_copy(b2_all[:, :, 1, :], b2_zero[:, :, :])
            plan.then(dve, nc.vector.tensor_copy(b2_hi[:, :, :], b2_raw[:, :, :]))
            nc.vector.scalar_tensor_tensor(out=b2_all[:, :, 0, :], in0=f32(b2_hi[:, :, :]), scalar=is_low[:, 0:1], in1=b2_raw[:, :, :],
                                           op0=ALU.mult, op1=ALU.add)

            def step(n, k):
                m = n - 1
                if there(m):
                    p = 1 - k
                    for h in range(2):
                        dve.wait_ge(y_low, 2 * m + h + 1)
                        if h == 0:
                            need(dve, y_stored[p], 8 * evens(m, p))
                        nc.vector.tensor_tensor(yo[p][:, 2 * h:2 * h + 2, :], Y[h][:, :].rearrange("p (t s d) -> p t s d", t=2, s=2)[:, :, 0, :],
                                                ylo[h][:, :, :], ALU.add).then_inc(yo_made, 1)
                m = n + 2
                if there(m):
                    dve.wait_ge(x_hi, m + 1)
                    nc.vector.tensor_tensor(xT_lo[k][:, :], XT[:, :], f32(xT_hi[k][:, :]), ALU.subtract).then_inc(x_lo, 1)
                    e = nc.values_load(of(tab_e, m), engines=[mybir.EngineType.DVE], min_val=0, max_val=E - 1)
                    need(dve, g_made, 2 * m - 2)
                    dve.sem_inc(e_passed, 1)
                    nc.vector.tensor_copy(bias1[k][:, :], b1_all[:, bass.ds(e, 1), :].rearrange("p o c -> p (o c)"))
                    nc.vector.tensor_copy(w1[k][:, :], f32(w1_all[:, bass.ds(e, 1), :].rearrange("p o c -> p (o c)"))).then_inc(w1_set, 1)
                m = n + 1
                if there(m):
                    p = 1 - k
                    dve.wait_ge(g_his[0], m + 1)
                    need(dve, down, 2 * m - 2)
                    nc.vector.tensor_tensor(g_lo[p][0][:, :], g[p][0][:, :], f32(g_hi[p][0][:, :]), ALU.subtract).then_inc(g_los, 1)
                    dve.wait_ge(g_his[1], m + 1)
                    nc.vector.tensor_tensor(g_lo[p][1][:, :], g[p][1][:, :], f32(g_hi[p][1][:, :]), ALU.subtract).then_inc(g_los, 1)
                if isinstance(n, int):
                    if n == -2:
                        weights.split_second_low(dve).then_inc(w_ready, 1)
                    if n in (-1, 0):
                        route.residual(dve, B - 1, n + 1, TR, LAST + n + 1)
                    if n == 1:
                        route.norm(dve, B - 1, LAST + 1)
                    if n == 8:
                        route.compare(dve, B - 1, TR, LAST + 4)
                    if n == 9:
                        route.break_ties(dve, B - 1)
                    if n == 10:
                        route.select(dve, B - 1)
                    if n == 12:
                        route.places(dve, B - 1, TR, LAST + 5)
                    if n == 13:
                        plan.converted(dve)
                        plan.first_tiles(dve, 1)
                    if n == 15:
                        plan.rows(dve, 1)

            def total(q, part):
                if part == PARTS:
                    return
                p = q % 2
                first, n = sum(PART_TILES[:part]), PART_TILES[part]
                t = slice(first, first + n)
                if part == 0:
                    dve.wait_ge(got_in[p], 256 * (q // 2 + 1))
                    need(dve, out_stored[p], 16 * (q // 2))
                nc.vector.tensor_tensor(fo[p][:, t, :], got[p][:, t, 0, :], got[p][:, t, 1, :], ALU.add).then_inc(summed, 1)
                dve.wait_ge(summed, PARTS * q + part + 1)
                nc.vector.tensor_tensor(fo[p][:, t, :], fo[p][:, t, :], x2[:, T * q + first:T * q + first + n, :], ALU.add).then_inc(fo_made, 1)

            loop(dve, step, total)

        @block.tensor
        def _(pe):
            route.count(pe, B - 2, TR, LAST - 1, True)
            pe.wait_ge(b_in, 48)
            nc.tensor.transpose(XT[:, 0:2 * E], b_raw[:, :], ident[0:2 * E, 0:2 * E]).then_inc(b_turned, 1)

            def step(n, k):
                m = n + 2
                if there(m):
                    pe.wait_ge(x_in[k], 16 + 8 * evens(m, k))
                    need(pe, x_lo, m)
                    if isinstance(m, int) and m == 0:
                        pe.wait_ge(b_taken, 1)
                    for t in range(CT):
                        ins = nc.tensor.transpose(XT[:, P * t:P * t + P], xg[k][:, t, :], ident[:, :])
                    ins.then_inc(xt_full, 1)
                m = n + 1
                if there(m):
                    p = 1 - k
                    pe.wait_ge(w1_set, m + 1)
                    pe.wait_ge(x_lo, m + 1)
                    for c in range(HC):
                        need(pe, g_made, 2 * m + c - 3)
                        hi, lo = w1[p][:, P * c:P * c + P], w1[p][:, HC * P + P * c:HC * P + P * c + P]
                        for i, (w, r) in enumerate(((hi, xT_hi), (hi, xT_lo), (lo, xT_hi))):
                            ins = nc.tensor.matmul(U[2 * p + c][:, :], w, r[p][:, :], start=(i == 0), stop=(i == 2))
                        ins.then_inc(u_full, 1)
                m = n
                if there(m):
                    e = nc.values_load(of(tab_e, m), engines=[mybir.EngineType.PE], min_val=0, max_val=E - 1)
                    if isinstance(m, int) and m == 0:
                        pe.wait_ge(w_ready, 1)
                    pe.wait_ge(g_los, 2 * m + 2)
                    for h in range(2):
                        need(pe, yo_made, 2 * m + h - 1)
                        pe.sem_inc(e_passed, 1)
                        nc.tensor.matmul(Y[h][:, :].rearrange("p (t w) -> p t w", t=2), ones_r[:, :],
                                         b2_all[:, bass.ds(e, 1), :, :].rearrange("p o s d -> p o (s d)").to_broadcast([2, 2, 2 * P]),
                                         start=True, stop=False)
                        for t in range(2):
                            rows = slice(P * (2 * h + t), P * (2 * h + t) + P)
                            for c in range(HC):
                                for gh in (g_hi, g_lo):
                                    ins = nc.tensor.matmul(Y[h][:, 2 * P * t:2 * P * t + 2 * P], gh[k][c][:, rows],
                                                           w2_all[:, bass.ds(e, 1), c, :, :].rearrange("p o s d -> p (o s d)"),
                                                           start=False, stop=(t == 1 and c == HC - 1 and gh is g_lo))
                        ins.then_inc(down, 1)
                if isinstance(n, int):
                    if n in (-2, -1):
                        c = n + 2
                        route.output_turn(pe, 6 * B - 2 + c, c, TR, LAST + c, True)
                    if n in (3, 5):
                        c = (n - 3) // 2
                        route.result_turn(pe, B - 1, 1, c, TR, LAST + c + 2, True)
                    if n == 7:
                        route.scores(pe, B - 1, TR, LAST + 4, True)
                    if n == 11:
                        route.count(pe, B - 1, TR, LAST + 5, True)

            loop(pe, step)


_INS = ['x', 'adj', 'L0_gnn_weight', 'L0_gnn_w_ih', 'L0_gnn_w_hh', 'L0_gnn_b_ih', 'L0_gnn_b_hh', 'L0_ffn_Wg',
        'L0_ffn_bg', 'L0_ffn_W1', 'L0_ffn_b1', 'L0_ffn_W2', 'L0_ffn_b2']


def kernel(**inputs):
    import numpy as _np
    import concourse.bacc as _bacc
    from concourse import mybir as _mybir
    from concourse.bass_utils import run_bass_kernel_spmd as _run

    nc = _bacc.Bacc("TRN2", target_bir_lowering=False, num_devices=1)
    arrays, args = {}, []
    for name in _INS:
        a = _np.ascontiguousarray(inputs[name])
        arrays[f"in_{name}_dram"] = a
        args.append(nc.dram_tensor(f"in_{name}_dram", a.shape, _mybir.dt.from_np(a.dtype), kind="ExternalInput").ap())
    args.append(nc.dram_tensor("out_0_dram", (8, 1024, 128), _mybir.dt.float32, kind="ExternalOutput").ap())
    gnn_ffn(nc, *args)
    r = _run(nc, [arrays], core_ids=[0])
    return r.results[0]["out_0_dram"]
```
